# Optimizing a Trainium2 kernel written in Bass

```python
import numpy as np
import jax
import jax.numpy as jnp

def _softmax(x, axis=-1):
    return jax.nn.softmax(x, axis=axis)

def _gelu(x):
    return jax.nn.gelu(x, approximate=True)

def _silu(x):
    return jax.nn.silu(x)

def _sigmoid(x):
    return jax.nn.sigmoid(x)

def _layernorm(x, axis=-1, eps=1e-05):
    m = jnp.mean(x, axis=axis, keepdims=True)
    v = jnp.var(x, axis=axis, keepdims=True)
    return (x - m) / jnp.sqrt(v + eps)

def _scatter_add(tgt, idx, src, axis=0):
    return tgt.at[idx].add(src)

def _segment_sum(src, seg, n):
    return jax.ops.segment_sum(src, seg, n)
kernel_name = 'mk_gnn_preln_d1_gnn_r8_a548f8'

def setup_inputs(seed: int=0):
    np.random.seed(seed)
    _w = jnp.asarray

    def _rec_inputs():
        import jax
        import jax.numpy as jnp
        _gk = jax.random.key(seed)
        x = -0.0002117 + 1 * jax.random.normal(jax.random.fold_in(_gk, 1), (6250, 256), jnp.float32)
        _s = jax.random.randint(jax.random.fold_in(_gk, 2), (100000,), 0, 6250, jnp.int32)
        _d = jax.random.randint(jax.random.fold_in(_gk, 3), (100000,), 0, 6250, jnp.int32)
        _loop = jnp.arange(6250, dtype=jnp.int32)
        src = jnp.concatenate([_s, _d, _loop])
        dst = jnp.concatenate([_d, _s, _loop])
        _o = jnp.argsort(dst, stable=True)
        src = src[_o]
        dst = dst[_o]
        edge_attr_32 = jax.random.uniform(jax.random.fold_in(_gk, 12), (206250, 32), jnp.float32, 0.0, 1)
        return (x, src, dst, edge_attr_32)
    x, src, dst, edge_attr_32 = _rec_inputs()

    def _L0_gnn_setup():
        import jax, jax.numpy as jnp
        import numpy as np
        N = 12500
        E = 200000
        D_NODE = 256
        D_MSG = 128
        D_RBF = 32
        H = 8
        D_HEAD = D_MSG // H
        key = jax.random.key(seed)
        ks = jax.random.split(key, 12)
        x = jax.random.normal(ks[0], (N, D_NODE), dtype=jnp.float32)
        rbf = jax.random.uniform(ks[1], (E, D_RBF), dtype=jnp.float32)
        dst = jax.random.randint(ks[2], (E,), 0, N)
        r = jax.random.randint(ks[3], (E,), 1, N)
        src = (dst + r) % N
        edge_index = jnp.stack([src, dst]).astype(jnp.int64)
        batch = jnp.zeros((N,), dtype=jnp.int64)
        s = 0.05
        W_n2m = jax.random.normal(ks[4], (D_MSG, D_NODE), dtype=jnp.float32) * s
        W_r2m = jax.random.normal(ks[5], (D_MSG, D_RBF), dtype=jnp.float32) * s
        Wl = jax.random.normal(ks[6], (D_MSG, D_MSG), dtype=jnp.float32) * s
        bl = jnp.zeros((D_MSG,), dtype=jnp.float32)
        Wr = jax.random.normal(ks[7], (D_MSG, D_MSG), dtype=jnp.float32) * s
        br = jnp.zeros((D_MSG,), dtype=jnp.float32)
        We = jax.random.normal(ks[8], (D_MSG, D_MSG), dtype=jnp.float32) * s
        att = jax.random.normal(ks[9], (H, D_HEAD), dtype=jnp.float32) * s
        bias = jnp.zeros((D_MSG,), dtype=jnp.float32)
        W_m2n = jax.random.normal(ks[10], (D_NODE, D_MSG), dtype=jnp.float32) * s
        return {'x': x, 'rbf': rbf, 'edge_index': edge_index, 'batch': batch, 'W_n2m': W_n2m, 'W_r2m': W_r2m, 'Wl': Wl, 'bl': bl, 'Wr': Wr, 'br': br, 'We': We, 'att': att, 'bias': bias, 'W_m2n': W_m2n}
    _L0_gnn_all = _L0_gnn_setup()
    _L0_gnn_in = {k: v for k, v in _L0_gnn_all.items() if k in ('W_n2m', 'W_r2m', 'Wl', 'bl', 'Wr', 'br', 'We', 'att', 'bias', 'W_m2n')}
    del _L0_gnn_all
    return {'x': x, 'src': src, 'dst': dst, 'edge_attr_32': edge_attr_32, 'L0_gnn_W_n2m': _L0_gnn_in['W_n2m'], 'L0_gnn_W_r2m': _L0_gnn_in['W_r2m'], 'L0_gnn_Wl': _L0_gnn_in['Wl'], 'L0_gnn_bl': _L0_gnn_in['bl'], 'L0_gnn_Wr': _L0_gnn_in['Wr'], 'L0_gnn_br': _L0_gnn_in['br'], 'L0_gnn_We': _L0_gnn_in['We'], 'L0_gnn_att': _L0_gnn_in['att'], 'L0_gnn_bias': _L0_gnn_in['bias'], 'L0_gnn_W_m2n': _L0_gnn_in['W_m2n']}

def reference(x, src, dst, edge_attr_32, L0_gnn_W_n2m, L0_gnn_W_r2m, L0_gnn_Wl, L0_gnn_bl, L0_gnn_Wr, L0_gnn_br, L0_gnn_We, L0_gnn_att, L0_gnn_bias, L0_gnn_W_m2n):
    import jax
    import jax.numpy as jnp

    def _L0_gnn_ref(x, rbf, edge_index, batch, W_n2m, W_r2m, Wl, bl, Wr, br, We, att, bias, W_m2n):
        import jax, jax.numpy as jnp
        import numpy as np
        N = 12500
        E = 200000
        D_NODE = 256
        D_MSG = 128
        D_RBF = 32
        H = 8
        D_HEAD = D_MSG // H
        n = x.shape[0]
        h, d = att.shape
        xm = x @ W_n2m.T
        ea = rbf @ W_r2m.T
        src, dst = (edge_index[0], edge_index[1])
        deg = jax.ops.segment_sum(jnp.ones((ea.shape[0],), ea.dtype), dst, num_segments=n)
        loop_attr = jax.ops.segment_sum(ea, dst, num_segments=n) / jnp.maximum(deg, 1.0)[:, None]
        loop_idx = jnp.arange(n, dtype=src.dtype)
        src_f = jnp.concatenate([src, loop_idx])
        dst_f = jnp.concatenate([dst, loop_idx])
        ea_f = jnp.concatenate([ea, loop_attr], axis=0)
        xl = (xm @ Wl.T + bl).reshape(n, h, d)
        xr = (xm @ Wr.T + br).reshape(n, h, d)
        e = (ea_f @ We.T).reshape(-1, h, d)
        u = jax.nn.leaky_relu(xl[src_f] + xr[dst_f] + e, 0.2)
        logits = jnp.einsum('ehd,hd->eh', u, att)
        mx = jax.ops.segment_max(logits, dst_f, num_segments=n)
        p = jnp.exp(logits - mx[dst_f])
        denom = jax.ops.segment_sum(p, dst_f, num_segments=n)
        alpha = p / denom[dst_f]
        msg = xl[src_f] * alpha[:, :, None]
        out = jax.ops.segment_sum(msg, dst_f, num_segments=n).reshape(n, h * d) + bias
        return out @ W_m2n.T
    edge_index = jnp.stack([src, dst])
    batch0 = jnp.zeros((6250,), jnp.int32)
    h = jnp.maximum(_layernorm(x, axis=-1), 0.0)
    x = x + _L0_gnn_ref(h, edge_attr_32, edge_index, batch0, L0_gnn_W_n2m, L0_gnn_W_r2m, L0_gnn_Wl, L0_gnn_bl, L0_gnn_Wr, L0_gnn_br, L0_gnn_We, L0_gnn_att, L0_gnn_bias, L0_gnn_W_m2n)
    return x

_drawn_inputs = setup_inputs


def setup_inputs(seed=0):
    import zlib

    import numpy as np

    out = dict(_drawn_inputs(seed))
    spreads = {'L0_gnn_bl': (0.0, 0.1), 'L0_gnn_br': (0.0, 0.8), 'L0_gnn_bias': (0.0, 0.1)}
    factors = {'edge_attr_32': 8.0,
     'L0_gnn_W_r2m': 8.0,
     'L0_gnn_Wr': 8.0,
     'L0_gnn_We': 8.0,
     'L0_gnn_att': 8.0}
    for name, (base, spread) in spreads.items():
        noise = np.random.default_rng([zlib.crc32(name.encode()), seed]).standard_normal(out[name].shape)
        drawn = base * np.exp(spread * noise) if base else spread * noise
        out[name] = jnp.asarray(drawn.astype(out[name].dtype))
    for name, factor in factors.items():
        out[name] = (out[name] * factor).astype(out[name].dtype)
    return out
```

```python
from contextlib import ExitStack

import numpy as np

import concourse.bass as bass
from concourse import mybir

FP32, I32 = mybir.dt.float32, mybir.dt.int32
ALU, ACT, AX = mybir.AluOpType, mybir.ActivationFunctionType, mybir.AxisListType

P = 128
N, D_NODE, D_MSG, D_RBF, HEADS = 6250, 256, 128, 32, 8
D_HEAD = D_MSG // HEADS
E = 206250
TILES = 4
GROUP = TILES * P
GROUPS = -(-E // GROUP)
OVERLAP = GROUPS * GROUP - E
WINDOWS = -(-N // P)
LAST_ROWS = N - (WINDOWS - 1) * P
STEPS = GROUPS + WINDOWS - 1
CHUNKS = -(-GROUPS // P)
ROW = D_MSG + HEADS
HC = D_HEAD + 1
MSG = HEADS * HC
CNT = MSG + 1
AGG = CNT + D_RBF
EXT = HEADS + 1
FILLED = 72
BIG = 1e30
NO_NODE = 1 << 20
X_LIMIT = 60.0
EPS = 1e-5
SLOPE = 0.2
RING = 8
OH_RING = 4
UNROLL = 8
META = 3 * TILES
XCHUNKS = 6
FB = 7
FBATCH = WINDOWS // FB
assert FB * FBATCH == WINDOWS



def sweep(eng, count, peel, unroll, start=0):
    loops = (count - peel) // unroll
    for k in range(start, peel):
        yield k, k % unroll, k // unroll
    with eng.Fori(0, loops) as b:
        for i in range(peel, peel + unroll):
            yield b * unroll + i, i % unroll, b + i // unroll
    for k in range(peel + loops * unroll, count):
        yield k, k % unroll, k // unroll


def inside(j, count):
    return not isinstance(j, int) or 0 <= j < count


def one(k):
    return slice(k, k + 1) if isinstance(k, int) else bass.DynSlice(k, 1)


def settled(eng, value):
    return value if isinstance(value, int) else eng.snap(eng.to_reg(value))


def at(tile, w):
    if isinstance(w, int):
        return tile[:, w]
    return tile[:, bass.DynSlice(w, 1), :].rearrange("p a d -> p (a d)")



def gat_kernel(nc, x, src, dst, edge_attr, W_n2m, W_r2m, Wl, bl, Wr, br, We, att, bias, W_m2n, out):
    xl_table = nc.dram_tensor("xl_table", (WINDOWS * P, ROW), FP32, kind="Internal").ap()
    meta_dram = nc.dram_tensor("meta_dram", (GROUPS, P, META), I32, kind="Internal").ap()
    starts_dram = nc.dram_tensor("starts_dram", (GROUPS, TILES, P), FP32, kind="Internal").ap()

    with ExitStack() as ctx:
        def sb(name, shape, dt=FP32):
            return ctx.enter_context(nc.sbuf_tensor(name, shape, dt))

        x_sb = sb("x_sb", [P, WINDOWS, D_NODE])
        xl_sb = sb("xl_sb", [P, WINDOWS, ROW])
        xr_sb = sb("xr_sb", [P, WINDOWS, ROW])
        ident = sb("ident", [P, P])
        iota_n = sb("iota_n", [P, P])
        att_relu = sb("att_relu", [P, D_MSG])
        Wc_diag = sb("Wc_diag", [P, TILES * ROW])
        W_outT = sb("W_outT", [P, D_NODE])
        bias_col = sb("bias_col", [P, 1])
        base_tab = sb("base_tab", [P, STEPS])
        win_tab = sb("win_tab", [1, STEPS], I32)
        grp_tab = sb("grp_tab", [1, STEPS], I32)
        edge_tab = sb("edge_tab", [1, STEPS], I32)

        banks = ctx.enter_context(nc.psum_tensor("banks", [P, 8, 512], FP32))

        prologue(nc, banks, xl_table, meta_dram, starts_dram,
                 (x, src, dst, W_n2m, W_r2m, Wl, bl, Wr, br, We, att, bias, W_m2n),
                 x_sb, xl_sb, xr_sb, ident, iota_n, att_relu, Wc_diag, W_outT, bias_col,
                 base_tab, win_tab, grp_tab, edge_tab)

        acc = sb("acc", [P, WINDOWS, AGG])
        node_max = sb("node_max", [P, WINDOWS, HEADS])
        edge_loop(nc, banks, xl_table, meta_dram, starts_dram, edge_attr,
                  xr_sb, ident, iota_n, att_relu, Wc_diag, base_tab, win_tab, grp_tab, edge_tab,
                  acc, node_max)
        finale(nc, banks, x_sb, xl_sb, xr_sb, ident, att_relu, Wc_diag, W_outT, bias_col,
               acc, node_max, out)


def prologue(nc, banks, xl_table, meta_dram, starts_dram, inputs,
             x_sb, xl_sb, xr_sb, ident, iota_n, att_relu, Wc_diag, W_outT, bias_col,
             base_tab, win_tab, grp_tab, edge_tab):
    x, src, dst, W_n2m, W_r2m, Wl, bl, Wr, br, We, att, bias, W_m2n = inputs
    full_w = WINDOWS - 1
    xc = full_w // XCHUNKS
    full_g = GROUPS - 1
    with ExitStack() as ctx:
        def sb(name, shape, dt=FP32):
            return ctx.enter_context(nc.sbuf_tensor(name, shape, dt))

        def sem(name):
            return ctx.enter_context(nc.semaphore(name))

        src_i = sb("src_i", [P, CHUNKS, GROUP], I32)
        dst_i = sb("dst_i", [P, CHUNKS, GROUP], I32)
        meta_b = sb("meta_b", [P, CHUNKS, P, META], I32)
        starts_b = sb("starts_b", [P, CHUNKS, TILES, P])
        masked = sb("masked", [1, OVERLAP], I32)
        lasts_i = sb("lasts_i", [1, GROUPS], I32)
        lasts = sb("lasts", [1, GROUPS])
        below = sb("below", [WINDOWS, GROUPS])
        count = sb("count", [WINDOWS, 1])
        first = sb("first", [WINDOWS, 1])
        first_step = sb("first_step", [WINDOWS, 1])
        begun = sb("begun", [WINDOWS, STEPS])
        walk = sb("walk", [1, 2, STEPS])
        ones = sb("ones", [P, P])
        iota_ni = sb("iota_ni", [P, P], I32)
        iota_si = sb("iota_si", [WINDOWS, STEPS], I32)
        iota_s = sb("iota_s", [WINDOWS, STEPS])
        iota_wi = sb("iota_wi", [P, 1], I32)
        iota_w = sb("iota_w", [P, 1])
        bound_w = sb("bound_w", [P, 1])
        W1 = sb("W1", [P, D_NODE])
        Wr2m = sb("Wr2m", [P, TILES, D_RBF])
        Wlre = sb("Wlre", [P, 3, D_MSG])
        WlreT = sb("WlreT", [P, 3, D_MSG])
        Wout = sb("Wout", [P, 2, D_MSG])
        Wall = sb("Wall", [P, 7, ROW])
        att_bc = sb("att_bc", [P, D_MSG])
        Watt = sb("Watt", [P, 7, D_MSG])
        Wshare = sb("Wshare", [P, 7, HEADS])
        lr_row = sb("lr_row", [1, 2 * D_MSG])
        att_row = sb("att_row", [1, D_MSG])
        bn = sb("bn", [P, 2, 6])
        mv = sb("mv", [P, WINDOWS, 2])
        var_eps = sb("var_eps", [P, WINDOWS])
        std = sb("std", [P, WINDOWS])
        rstd = sb("rstd", [P, WINDOWS])
        shift = sb("shift", [P, WINDOWS])
        h = sb("h", [P, 2, D_NODE])
        hT = sb("hT", [P, 2, D_NODE])

        x_in = [sem(f"x_in{i}") for i in range(XCHUNKS + 1)]
        weights_in, groups_in, lasts_in, table_out = map(sem, ("weights_in", "groups_in", "lasts_in", "table_out"))
        ones_ready, ident_zero, ident_ready, iotas_int, iotas_ready, mask_ready, x_tail_zero, diag_zero = map(
            sem, ("ones_ready", "ident_zero", "ident_ready", "iotas_int", "iotas_ready", "mask_ready",
                  "x_tail_zero", "diag_zero"))
        wT_done, wT_ready, w_prod, w_copied, w_att, w_sum, w_share, w_ready = map(
            sem, ("wT_done", "wT_ready", "w_prod", "w_copied", "w_att", "w_sum", "w_share", "w_ready"))
        meta_ready, runs_ready, flags_ready = map(sem, ("meta_ready", "runs_ready", "flags_ready"))
        lasts_ready, lasts_spread, counted, clipped, first_ready, begun_ready, walk_spread, walk_done, grp_done, \
            tabs_ready = map(sem, ("lasts_ready", "lasts_spread", "counted", "clipped", "first_ready",
                                   "begun_ready", "walk_spread", "walk_done", "grp_done", "tabs_ready"))
        bn_done, mv_done, var_done, std_done, rstd_done, shift_done = map(
            sem, ("bn_done", "mv_done", "var_done", "std_done", "rstd_done", "shift_done"))
        h_ready, hT_done, hT_ready, proj_done, xl_ready, xr_ready = map(
            sem, ("h_ready", "hT_done", "hT_ready", "proj_done", "xl_ready", "xr_ready"))
        block = ctx.enter_context(nc.Block())

        hT_ps, proj_ps = [banks[:, i] for i in (0, 1)], [banks[:, i] for i in (2, 3)]
        wps, cps = [banks[:, i] for i in (4, 5)], banks[:, 6]
        n_weights = 5 + TILES + 4

        @block.sync
        def _(sp):
            xw = x[0:full_w * P, :].rearrange("(w p) d -> p w d", p=P)
            for c in range(XCHUNKS):
                sp.dma_start(x_sb[:, c * xc:(c + 1) * xc, :], xw[:, c * xc:(c + 1) * xc, :]).then_inc(x_in[c], 16)
            sp.wait_ge(x_tail_zero, 1)
            sp.dma_start(x_sb[0:LAST_ROWS, full_w, :], x[full_w * P:N, :]).then_inc(x_in[XCHUNKS], 16)
            sp.wait_ge(flags_ready, CHUNKS)
            for c in range(CHUNKS):
                r = min(P, GROUPS - c * P)
                sp.dma_start(meta_dram[c * P:c * P + r], meta_b[0:r, c]).then_inc(table_out, 16)
                sp.dma_start(starts_dram[c * P:c * P + r], starts_b[0:r, c]).then_inc(table_out, 16)
            for b in range(FBATCH):
                sp.wait_ge(xl_ready, (b + 1) * FB)
                sp.dma_start(xl_table[b * FB * P:(b + 1) * FB * P, :].rearrange("(w p) d -> p w d", p=P),
                             xl_sb[:, b * FB:(b + 1) * FB, :]).then_inc(table_out, 16)
            sp.wait_ge(table_out, 16 * (2 * CHUNKS + FBATCH))

        @block.gpsimd
        def _(pool):
            nc.gpsimd.memset(ones[:], 1.0).then_inc(ones_ready, 1)
            nc.gpsimd.memset(ident[:], 0.0).then_inc(ident_zero, 1)
            nc.gpsimd.memset(x_sb[:, full_w, :], 0.0).then_inc(x_tail_zero, 1)
            nc.gpsimd.memset(masked[:], NO_NODE).then_inc(mask_ready, 1)
            nc.gpsimd.iota(iota_ni[:], pattern=[[1, P]], base=0, channel_multiplier=0).then_inc(iotas_int, 1)
            nc.gpsimd.iota(iota_si[:], pattern=[[1, STEPS]], base=0, channel_multiplier=0).then_inc(iotas_int, 1)
            nc.gpsimd.iota(iota_wi[:], pattern=[[0, 1]], base=0, channel_multiplier=1).then_inc(iotas_int, 1)
            pool.wait_ge(ident_zero, 1)
            nc.gpsimd.affine_select(out=ident[:], in_=ident[:], compare_op=ALU.not_equal, fill=1.0, base=0,
                                    pattern=[[-1, P]], channel_multiplier=1).then_inc(ident_ready, 1)
            nc.gpsimd.memset(Wc_diag[:], 0.0).then_inc(diag_zero, 1)

        @block.scalar
        def _(act):
            for c in range(CHUNKS):
                r = min(P, full_g - c * P)
                for to, of in ((src_i, src), (dst_i, dst)):
                    act.dma_start(to[0:r, c], of[c * P * GROUP:(c * P + r) * GROUP].rearrange("(g k) -> g k", k=GROUP)
                                  ).then_inc(groups_in, 16)
            tail = full_g - (CHUNKS - 1) * P
            act.dma_start(src_i[tail:tail + 1, CHUNKS - 1], src[E - GROUP:E].rearrange("(a k) -> a k", a=1)
                          ).then_inc(groups_in, 16)
            act.dma_start(dst_i[tail:tail + 1, CHUNKS - 1, OVERLAP:], dst[E - GROUP + OVERLAP:E].rearrange(
                "(a k) -> a k", a=1)).then_inc(groups_in, 16)
            act.wait_ge(mask_ready, 1)
            act.dma_start(dst_i[tail:tail + 1, CHUNKS - 1, 0:OVERLAP], masked[:]).then_inc(groups_in, 16)
            act.dma_start(lasts_i[0:1, 0:full_g], dst[0:full_g * GROUP].rearrange("(g k) -> k g", k=GROUP)[
                GROUP - 1:GROUP, :], allow_slow_non_contiguous=True).then_inc(lasts_in, 16)
            act.dma_start(lasts_i[0:1, full_g:GROUPS], dst[E - 1:E].rearrange("(a k) -> a k", a=1)
                          ).then_inc(lasts_in, 16)
            act.dma_start(W1[:], W_n2m).then_inc(weights_in, 16)
            for i, w in enumerate((Wl, Wr, We)):
                act.dma_start(Wlre[:, i], w).then_inc(weights_in, 16)
            for t in range(TILES):
                act.dma_start(Wr2m[:, t], W_r2m).then_inc(weights_in, 16)
            act.dma_start(Wout[:], W_m2n.rearrange("(c p) m -> p c m", p=P)).then_inc(weights_in, 16)
            act.dma_start(lr_row[0:1, 0:D_MSG], bl.rearrange("(a k) -> a k", a=1)).then_inc(weights_in, 16)
            act.dma_start(lr_row[0:1, D_MSG:], br.rearrange("(a k) -> a k", a=1)).then_inc(weights_in, 16)
            act.dma_start(att_row[0:1, :].rearrange("a (h d) -> a h d", h=HEADS),
                          att.rearrange("(a h) d -> a h d", a=1)).then_inc(weights_in, 16)
            act.dma_start(bias_col[:], bias.rearrange("(p a) -> p a", a=1)).then_inc(weights_in, 16)
            act.wait_ge(var_done, 1)
            nc.scalar.activation(std[:], var_eps[:], ACT.Sqrt).then_inc(std_done, 1)

            act.wait_ge(shift_done, 1)

            def normal(w, s):
                if inside(w - 2, WINDOWS):
                    act.wait_ge(hT_done, w - 1)
                nc.scalar.activation(h[:, s], at(x_sb, w), ACT.Relu, bias=shift[:, one(w)],
                                     scale=rstd[:, one(w)]).then_inc(h_ready, 1)

            normal(0, 0)
            for w, s, _ in sweep(act, WINDOWS, 2, 2):
                if inside(w + 1, WINDOWS):
                    normal(w + 1, 1 - s)
                act.wait_ge(proj_done, w + 1)
                nc.scalar.activation(at(xl_sb, w), proj_ps[s][:, 0:ROW], ACT.Copy).then_inc(xl_ready, 1)
                nc.scalar.activation(at(xr_sb, w), proj_ps[s][:, ROW:2 * ROW], ACT.Copy).then_inc(xr_ready, 1)

        @block.tensor
        def _(pe):
            pe.wait_ge(ident_ready, 1)
            pe.wait_ge(weights_in, 16 * n_weights)
            pe.wait_ge(ones_ready, 1)
            for i in range(3):
                nc.tensor.transpose(wps[0][:, i * P:(i + 1) * P], Wlre[:, i], ident[:]).then_inc(wT_done, 1)
            for i in range(2):
                nc.tensor.transpose(wps[1][:, i * P:(i + 1) * P], Wout[:, i], ident[:]).then_inc(wT_done, 1)
            pe.wait_ge(lasts_ready, 1)
            nc.tensor.matmul(cps[0:WINDOWS, 0:GROUPS], ones[0:1, 0:WINDOWS], lasts[:], start=True, stop=True
                             ).then_inc(lasts_spread, 1)
            pe.wait_ge(wT_ready, 2)
            for c in range(2):
                for i in range(2):
                    nc.tensor.matmul(wps[0][:, (2 * c + i) * P:(2 * c + i + 1) * P], W1[:, c * P:(c + 1) * P],
                                     WlreT[:, i], start=True, stop=True).then_inc(w_prod, 1)
            nc.tensor.matmul(wps[1][:, 0:D_MSG], Wr2m[:].rearrange("p t k -> p (t k)"), WlreT[:, 2],
                             start=True, stop=True).then_inc(w_prod, 1)
            nc.tensor.matmul(wps[1][:, D_MSG:2 * D_MSG], ones[0:1, :], att_row[:], start=True, stop=True
                             ).then_inc(w_prod, 1)
            pe.wait_ge(begun_ready, 1)
            nc.tensor.matmul(cps[:, 0:STEPS], ones[0:WINDOWS, :], begun[:], start=True, stop=True
                             ).then_inc(walk_spread, 1)
            pe.wait_ge(w_share, 1)

            def flip(w, s):
                pe.wait_ge(h_ready, w + 1)
                if inside(w - 2, WINDOWS):
                    pe.wait_ge(hT_ready, w - 1)
                nc.tensor.transpose(hT_ps[s][:, 0:P], h[:, s, 0:P], ident[:])
                nc.tensor.transpose(hT_ps[s][:, P:2 * P], h[:, s, P:2 * P], ident[:]).then_inc(hT_done, 1)

            flip(0, 0)
            for w, s, _ in sweep(pe, WINDOWS, 2, 2):
                if inside(w + 1, WINDOWS):
                    flip(w + 1, 1 - s)
                pe.wait_ge(hT_ready, w + 1)
                if inside(w - 2, WINDOWS):
                    pe.wait_ge(xl_ready, w - 1)
                    pe.wait_ge(xr_ready, w - 1)
                lr = proj_ps[s][:, 0:2 * ROW]
                w_of = Wall[:].rearrange("p b r -> p (b r)")
                nc.tensor.matmul(lr, ones[0:1, :], w_of[0:1, 4 * ROW:6 * ROW], start=True, stop=False)
                nc.tensor.matmul(lr, hT[:, s, 0:P], w_of[:, 0:2 * ROW], start=False, stop=False)
                nc.tensor.matmul(lr, hT[:, s, P:2 * P], w_of[:, 2 * ROW:4 * ROW], start=False, stop=True
                                 ).then_inc(proj_done, 1)

        @block.vector
        def _(dve):
            for w in range(WINDOWS):
                if w % xc == 0:
                    dve.wait_ge(x_in[w // xc], 16)
                nc.vector.bn_stats(bn[:, w % 2], x_sb[:, w]).then_inc(bn_done, 1)
                dve.wait_ge(bn_done, w + 1)
                nc.vector.bn_aggr(mv[:, w], bn[:, w % 2]).then_inc(mv_done, 1)
            dve.wait_ge(mv_done, WINDOWS)
            nc.vector.tensor_scalar(var_eps[:], mv[:, :, 1], EPS, None, ALU.add).then_inc(var_done, 1)
            dve.wait_ge(iotas_int, 3)
            nc.vector.tensor_copy(iota_n[:], iota_ni[:]).then_inc(iotas_ready, 1)
            nc.vector.tensor_copy(iota_s[:], iota_si[:]).then_inc(iotas_ready, 1)
            nc.vector.tensor_copy(iota_w[:], iota_wi[:]).then_inc(iotas_ready, 1)
            dve.wait_ge(iotas_ready, 3)
            nc.vector.tensor_scalar(bound_w[:], iota_w[:], float(P), None, ALU.mult).then_inc(iotas_ready, 1)
            dve.wait_ge(lasts_in, 32)
            nc.vector.tensor_copy(lasts[:], lasts_i[:]).then_inc(lasts_ready, 1)
            dve.wait_ge(std_done, 1)
            nc.vector.reciprocal(rstd[:], std[:]).then_inc(rstd_done, 1)
            dve.wait_ge(rstd_done, 1)
            nc.vector.scalar_tensor_tensor(out=shift[:], in0=mv[:, :, 0], scalar=-1.0, in1=rstd[:],
                                           op0=ALU.mult, op1=ALU.mult).then_inc(shift_done, 1)
            dve.wait_ge(wT_done, 5)
            nc.vector.tensor_copy(WlreT[:].rearrange("p i d -> p (i d)"), wps[0][:, 0:3 * P]).then_inc(wT_ready, 1)
            nc.vector.tensor_copy(W_outT[:], wps[1][:, 0:2 * P]).then_inc(wT_ready, 1)
            dve.wait_ge(w_prod, 6)
            dve.wait_ge(diag_zero, 1)
            nc.vector.memset(Wall[:, 4:6], 0.0).then_inc(w_copied, 1)
            nc.vector.tensor_copy(Wall[:, 0:4, 0:D_MSG], wps[0][:, 0:4 * P].rearrange("p (b d) -> p b d", b=4)
                                  ).then_inc(w_copied, 1)
            nc.vector.tensor_copy(Wall[:, 6, 0:D_MSG], wps[1][:, 0:D_MSG]).then_inc(w_copied, 1)
            nc.vector.tensor_copy(att_bc[:], wps[1][:, D_MSG:2 * D_MSG]).then_inc(w_copied, 1)
            nc.vector.tensor_scalar(att_relu[:], wps[1][:, D_MSG:2 * D_MSG], 1.0 - SLOPE, None, ALU.mult
                                    ).then_inc(w_copied, 1)
            dve.wait_ge(w_copied, 5)
            nc.vector.tensor_copy(Wall[0:1, 4:6, 0:D_MSG], lr_row[:].rearrange("p (b d) -> p b d", b=2)
                                  ).then_inc(w_copied, 1)
            dve.wait_ge(w_copied, 6)
            nc.vector.tensor_tensor(Watt[:], Wall[:, :, 0:D_MSG], att_bc[:].unsqueeze(1).broadcast_to([P, 7, D_MSG]),
                                    ALU.mult).then_inc(w_att, 1)
            dve.wait_ge(w_att, 1)
            nc.vector.tensor_reduce(Wshare[:], Watt[:].rearrange("p b (h d) -> p b h d", h=HEADS), AX.X, ALU.add
                                    ).then_inc(w_sum, 1)
            dve.wait_ge(w_sum, 1)
            nc.vector.tensor_scalar(Wall[:, :, D_MSG:ROW], Wshare[:], SLOPE, None, ALU.mult).then_inc(w_share, 1)
            dve.wait_ge(w_share, 1)
            for t in range(TILES):
                q = slice(t * D_RBF, (t + 1) * D_RBF)
                nc.vector.tensor_copy(Wc_diag[q, t * ROW:(t + 1) * ROW], Wall[q, 6]).then_inc(w_ready, 1)
            dve.wait_ge(lasts_spread, 1)
            dve.wait_ge(iotas_ready, 4)
            nc.vector.tensor_scalar(below[:], cps[0:WINDOWS, 0:GROUPS], bound_w[0:WINDOWS], None, ALU.is_lt
                                    ).then_inc(counted, 1)
            dve.wait_ge(counted, 1)
            nc.vector.reduce_sum(count[:], below[:], AX.X).then_inc(counted, 1)
            dve.wait_ge(counted, 2)
            nc.vector.tensor_scalar(first[:], count[:], float(GROUPS - 1), None, ALU.min).then_inc(clipped, 1)
            dve.wait_ge(clipped, 1)
            nc.vector.tensor_tensor(first_step[:], first[:], iota_w[0:WINDOWS], ALU.add).then_inc(first_ready, 1)
            dve.wait_ge(first_ready, 1)
            nc.vector.tensor_scalar(begun[:], iota_s[:], first_step[:], None, ALU.is_ge).then_inc(begun_ready, 1)
            dve.wait_ge(walk_spread, 1)
            nc.vector.tensor_scalar(base_tab[:], cps[:, 0:STEPS], -1.0, float(P), ALU.add, ALU.mult).then_inc(tabs_ready, 1)
            nc.vector.tensor_scalar(walk[0:1, 0], cps[0:1, 0:STEPS], -1.0, None, ALU.add).then_inc(walk_done, 1)
            dve.wait_ge(walk_done, 1)
            nc.vector.tensor_copy(win_tab[:], walk[0:1, 0]).then_inc(tabs_ready, 1)
            nc.vector.tensor_tensor(walk[0:1, 1], iota_s[0:1, :], walk[0:1, 0], ALU.subtract).then_inc(grp_done, 1)
            dve.wait_ge(grp_done, 1)
            nc.vector.tensor_copy(grp_tab[:], walk[0:1, 1]).then_inc(tabs_ready, 1)
            nc.vector.tensor_scalar(edge_tab[:], walk[0:1, 1], float(GROUP), float(E - GROUP), ALU.mult, ALU.min
                                    ).then_inc(tabs_ready, 1)
            for w, s, _ in sweep(dve, WINDOWS, 2, 2):
                dve.wait_ge(hT_done, w + 1)
                nc.vector.tensor_copy(hT[:, s], hT_ps[s][:, 0:2 * P]).then_inc(hT_ready, 1)
            dve.wait_ge(groups_in, 16 * (2 * CHUNKS + 3))
            for c in range(CHUNKS):
                r = min(P, GROUPS - c * P)
                m = meta_b[0:r, c]
                d = m[:, :, TILES:2 * TILES].bitcast(FP32)
                e = m[:, :, 2 * TILES:META].bitcast(FP32)
                nc.vector.tensor_copy(m[:, :, 0:TILES], src_i[0:r, c].rearrange("g (p t) -> g p t", t=TILES)
                                      ).then_inc(meta_ready, 1)
                nc.vector.tensor_copy(d, dst_i[0:r, c].rearrange("g (p t) -> g p t", t=TILES)).then_inc(meta_ready, 1)
                nc.vector.memset(e[:, P - 1, :], 1.0).then_inc(meta_ready, 1)
                nc.vector.memset(starts_b[0:r, c, :, 0], 0.0).then_inc(meta_ready, 1)
                dve.wait_ge(meta_ready, 4 * c + 4)
                nc.vector.tensor_tensor(e[:, 0:P - 1, :], d[:, 1:P, :], d[:, 0:P - 1, :], ALU.not_equal
                                        ).then_inc(runs_ready, 1)
                dve.wait_ge(runs_ready, c + 1)
                nc.vector.tensor_scalar(starts_b[0:r, c, :, 1:P].rearrange("g t p -> g p t"), e[:, 0:P - 1, :],
                                        -BIG, None, ALU.mult).then_inc(flags_ready, 1)


def edge_loop(nc, banks, xl_table, meta_dram, starts_dram, edge_attr,
              xr_sb, ident, iota_n, att_relu, Wc_diag, base_tab, win_tab, grp_tab, edge_tab, acc, node_max):
    with ExitStack() as ctx:
        def sb(name, shape, dt=FP32):
            return ctx.enter_context(nc.sbuf_tensor(name, shape, dt))

        def sem(name):
            return ctx.enter_context(nc.semaphore(name))

        meta = sb("meta", [P, RING, META], I32)
        rbf = sb("rbf", [P, RING, TILES * D_RBF])
        starts = sb("starts", [TILES * EXT, RING, P])
        xl_g = sb("xl_g", [P, RING, TILES, ROW])
        onehot = sb("onehot", [P, OH_RING, TILES, P])
        onehotT = sb("onehotT", [P, 2, GROUP])
        rbfT = sb("rbfT", [P, 2, P])
        u_att = sb("u_att", [P, TILES, D_MSG])
        u_sum = sb("u_sum", [P, TILES, HEADS])
        logit_all = sb("logit_all", [P, 2, FILLED])
        logit = [logit_all[:, i, 0:TILES * EXT].rearrange("p (t e) -> p t e", e=EXT) for i in (0, 1)]
        run_all = sb("run_all", [FILLED, P])
        run_max = run_all[0:TILES * EXT, :]
        last_max = sb("last_max", [P, TILES, EXT])
        absent = sb("absent", [P, TILES])
        tile_max = sb("tile_max", [P, TILES, HEADS])
        step_max = sb("step_max", [P, HEADS])
        new_max = sb("new_max", [P, 2, HEADS])
        fall = sb("fall", [P, 2, HEADS])
        shrink = sb("shrink", [P, 2, HEADS])
        above = sb("above", [P, TILES, HEADS])
        centred = sb("centred", [P, 2, TILES, HEADS])
        msg = sb("msg", [P, 2, TILES, CNT])

        z_ps = [banks[:, 2 * i:2 * i + 2].rearrange("p b (t d) -> p (b t) d", t=2) for i in (0, 1)]
        ohT_ps = banks[:, 4]
        rbfT_ps = banks[:, 5, 0:P]
        LT_ps = banks[0:TILES * EXT, 6, 2 * P:3 * P]
        FT_ps = banks[:, 6, 3 * P:3 * P + FILLED]
        F_ps = FT_ps[:, 0:TILES * EXT]
        ext_ps = banks[:, 6, 0:TILES * EXT].rearrange("p (t e) -> p t e", e=EXT)
        M_ps = banks[:, 6, P:P + TILES * HEADS].rearrange("p (t h) -> p t h", h=HEADS)
        U_ps = [banks[:, 7, i:i + AGG] for i in (0, 256)]

        loads = [sem(f"loads{i}") for i in range(RING)]
        gathers = [sem(f"gathers{i}") for i in range(RING)]
        state_ready = sem("state_ready")
        (oh_ready, ohT_done, ohT_ready, rbfT_done, rbfT_ready, z_done, att_done, sum_done, logit_ready, LT_done,
         scan_done, F_done, last_ready, ext_done, absent_done, tile_done, step_done, max_ready, fall_ready,
         max_kept, M_done, above_done, centred_ready, weight_ready, shrink_ready, msg_ready, agg_done,
         scaled, added) = map(sem, (
             "oh_ready", "ohT_done", "ohT_ready", "rbfT_done", "rbfT_ready", "z_done", "att_done", "sum_done",
             "logit_ready", "LT_done", "scan_done", "F_done", "last_ready", "ext_done", "absent_done",
             "tile_done", "step_done", "max_ready", "fall_ready", "max_kept", "M_done", "above_done",
             "centred_ready", "weight_ready", "shrink_ready", "msg_ready", "agg_done", "scaled", "added"))
        block = ctx.enter_context(nc.Block())
        FULL = 48

        @block.sync
        def _(sp):
            for k, s, r in sweep(sp, STEPS, RING, UNROLL):
                if inside(k - RING, STEPS):
                    sp.wait_ge(agg_done, k - RING + 1)
                g = sp.value_load(grp_tab[0:1, one(k)], min_val=0, max_val=GROUPS - 1)
                e = sp.value_load(edge_tab[0:1, one(k)], min_val=0, max_val=E - GROUP)
                sp.dma_start(meta[:, s], meta_dram[bass.DynSlice(g, 1)].rearrange("g p m -> p (g m)")
                             ).then_inc(loads[s], 16)
                sp.dma_start(rbf[:, s], edge_attr[bass.DynSlice(e, GROUP), :].rearrange("(p t) k -> p (t k)", t=TILES)
                             ).then_inc(loads[s], 16)
                row = starts_dram[bass.DynSlice(g, 1)].rearrange("g t p -> t g p")
                sp.dma_start(starts[:, s], row.broadcast_to([TILES, EXT, P])).then_inc(loads[s], 16)

        @block.gpsimd
        def _(pool):
            nc.gpsimd.memset(acc[:], 0.0).then_inc(state_ready, 1)
            nc.gpsimd.memset(node_max[:], -BIG).then_inc(state_ready, 1)
            nc.gpsimd.memset(logit_all[:], 1.0).then_inc(state_ready, 1)
            nc.gpsimd.memset(run_all[:], 0.0).then_inc(state_ready, 1)
            nc.gpsimd.memset(msg[:, :, :, MSG:CNT], 1.0).then_inc(state_ready, 1)
            for k, s, r in sweep(pool, STEPS, RING, UNROLL):
                full = settled(pool, (r + 1) * FULL)
                pool.wait_ge(state_ready, 5)
                pool.wait_ge(loads[s], full)
                for t in range(TILES):
                    pool.indirect_dma_start(out=xl_g[:, s, t], out_offset=None, in_=xl_table,
                                            in_offset=bass.IndirectOffsetOnAxis(ap=meta[:, s, t:t + 1], axis=0)
                                            ).then_inc(gathers[s], 16)

        @block.tensor
        def _(pe):
            pe.wait_ge(state_ready, 5)

            for k, s, r in sweep(pe, STEPS + 1, 2, UNROLL, start=-1):
                n, n_s, n_r = k + 1, (s + 1) % RING, r + (s + 1) // RING
                o, o_s = k - 1, (s - 1) % RING
                if inside(k, STEPS):
                    done = settled(pe, k + 1)
                    pe.wait_ge(state_ready, 5)
                    pe.wait_ge(logit_ready, done)
                    nc.tensor.transpose(banks[0:FILLED, 6, 2 * P:3 * P], logit_all[:, s % 2], ident[:]
                                        ).then_inc(LT_done, 1)
                if inside(n, STEPS):
                    pe.wait_ge(loads[n_s], (n_r + 1) * FULL)
                    if inside(n - 1, STEPS):
                        pe.wait_ge(rbfT_ready, n)
                    nc.tensor.transpose(rbfT_ps, rbf[:, n_s], ident[:]).then_inc(rbfT_done, 1)
                    pe.wait_ge(oh_ready, n + 1)
                    if inside(n - 1, STEPS):
                        pe.wait_ge(ohT_ready, n)
                    for t in range(TILES):
                        last = nc.tensor.transpose(ohT_ps[:, t * P:(t + 1) * P], onehot[:, n_s % OH_RING, t], ident[:])
                    last.then_inc(ohT_done, 1)
                    pe.wait_ge(gathers[n_s], (n_r + 1) * (16 * TILES))
                    if inside(n - 2, STEPS):
                        pe.wait_ge(logit_ready, n - 1)
                    for t in range(0, TILES, 2):
                        nc.tensor.matmul(z_ps[n_s % 2][:, t:t + 2, 0:ROW], ident[:], xl_g[:, n_s, t:t + 2],
                                         start=True, stop=False)
                if inside(k, STEPS):
                    pe.wait_ge(scan_done, k + 1)
                    nc.tensor.transpose(FT_ps, run_all[:], ident[0:FILLED, 0:FILLED]).then_inc(F_done, 1)
                if inside(n, STEPS):
                    pe.wait_ge(rbfT_ready, n + 1)
                    for t in range(0, TILES, 2):
                        nc.tensor.matmul(z_ps[n_s % 2][:, t:t + 2, 0:ROW], rbfT[:, n_s % 2],
                                         Wc_diag[:, t * ROW:(t + 2) * ROW], start=False, stop=False)
                if inside(k, STEPS):
                    pe.wait_ge(last_ready, k + 1)
                    if inside(k - 1, STEPS):
                        pe.wait_ge(tile_done, k)
                    for t in range(TILES):
                        last = nc.tensor.matmul(ext_ps[:, t], onehot[:, s % OH_RING, t], last_max[:, t],
                                                start=True, stop=True)
                    last.then_inc(ext_done, 1)
                if inside(o, STEPS):
                    pe.wait_ge(msg_ready, o + 1)
                    if inside(o - 2, STEPS):
                        pe.wait_ge(added, o - 1)
                    for t in range(TILES):
                        nc.tensor.matmul(U_ps[o_s % 2][:, 0:CNT], onehot[:, o_s % OH_RING, t], msg[:, o_s % 2, t],
                                         start=t == 0, stop=t == TILES - 1)
                    for t in range(TILES):
                        last = nc.tensor.matmul(U_ps[o_s % 2][:, CNT:AGG], onehot[:, o_s % OH_RING, t],
                                                rbf[:, o_s, t * D_RBF:(t + 1) * D_RBF],
                                                start=t == 0, stop=t == TILES - 1)
                    last.then_inc(agg_done, 1)
                if inside(n, STEPS):
                    w = pe.value_load(win_tab[0:1, one(n)], min_val=0, max_val=WINDOWS - 1)
                    pe.wait_ge(ohT_ready, n + 1)
                    for t in range(TILES):
                        last = nc.tensor.matmul(z_ps[n_s % 2][:, t, 0:ROW],
                                                onehotT[:, n_s % 2, t * P:(t + 1) * P], at(xr_sb, w),
                                                start=False, stop=t % 2 == 1)
                    last.then_inc(z_done, 1)
                if inside(k, STEPS):
                    pe.wait_ge(max_ready, k + 1)
                    if inside(k - 1, STEPS):
                        pe.wait_ge(above_done, k)
                    for t in range(TILES):
                        last = nc.tensor.matmul(M_ps[:, t], onehotT[:, s % 2, t * P:(t + 1) * P], new_max[:, s % 2],
                                                start=True, stop=True)
                    last.then_inc(M_done, 1)

        @block.scalar
        def _(act):
            act.wait_ge(state_ready, 5)
            for k, s, r in sweep(act, STEPS + 1, 2, UNROLL, start=-1):
                n, n_s = k + 1, (s + 1) % RING
                o, o_s = k - 1, (s - 1) % RING
                if inside(o, STEPS):
                    act.wait_ge(centred_ready, o + 1)
                    if inside(o - 2, STEPS):
                        act.wait_ge(agg_done, o - 1)
                    nc.scalar.activation(msg[:, o_s % 2, :, 0:MSG].rearrange("p t (h c) -> p t h c", c=HC)[:, :, :, D_HEAD],
                                         centred[:, o_s % 2], ACT.Exp).then_inc(weight_ready, 1)
                    act.wait_ge(fall_ready, o + 1)
                    if inside(o - 2, STEPS):
                        act.wait_ge(scaled, o - 1)
                    nc.scalar.activation(shrink[:, o_s % 2], fall[:, o_s % 2], ACT.Exp).then_inc(shrink_ready, 1)
                if inside(n, STEPS):
                    act.wait_ge(rbfT_done, n + 1)
                    if inside(n - 2, STEPS):
                        act.wait_ge(z_done, n - 1)
                    nc.scalar.activation(rbfT[:, n_s % 2], rbfT_ps, ACT.Copy).then_inc(rbfT_ready, 1)
                    act.wait_ge(ohT_done, n + 1)
                    if inside(n - 2, STEPS):
                        act.wait_ge(M_done, n - 1)
                    nc.scalar.activation(onehotT[:, n_s % 2], ohT_ps, ACT.Copy).then_inc(ohT_ready, 1)

        @block.vector
        def _(dve):
            dve.wait_ge(state_ready, 5)
            for k, s, r in sweep(dve, STEPS + 1, 2, UNROLL, start=-1):
                n, n_s, n_r = k + 1, (s + 1) % RING, r + (s + 1) // RING
                o, o_s = k - 1, (s - 1) % RING
                if inside(n, STEPS):
                    dve.wait_ge(loads[n_s], (n_r + 1) * FULL)
                    if inside(n - OH_RING, STEPS):
                        dve.wait_ge(agg_done, n - OH_RING + 1)
                    d = meta[:, n_s, TILES:2 * TILES].bitcast(FP32)
                    nc.vector.scalar_tensor_tensor(
                        out=onehot[:, n_s % OH_RING], in0=d.unsqueeze(2).broadcast_to([P, TILES, P]),
                        scalar=base_tab[:, one(n)], in1=iota_n[:].unsqueeze(1).broadcast_to([P, TILES, P]),
                        op0=ALU.subtract, op1=ALU.is_equal).then_inc(oh_ready, 1)
                if inside(k, STEPS):
                    dve.wait_ge(z_done, k + 1)
                    if inside(k - 1, STEPS):
                        dve.wait_ge(sum_done, k)
                    nc.vector.scalar_tensor_tensor(out=u_att[:], in0=z_ps[s % 2][:, :, 0:D_MSG], scalar=0.0,
                                                   in1=att_relu[:].unsqueeze(1).broadcast_to([P, TILES, D_MSG]),
                                                   op0=ALU.max, op1=ALU.mult).then_inc(att_done, 1)
                    dve.wait_ge(att_done, k + 1)
                    nc.vector.tensor_reduce(u_sum[:], u_att[:].rearrange("p t (h d) -> p t h d", d=D_HEAD),
                                            AX.X, ALU.add).then_inc(sum_done, 1)
                    dve.wait_ge(sum_done, k + 1)
                    if inside(k - 2, STEPS):
                        dve.wait_ge(LT_done, k - 1)
                    nc.vector.tensor_tensor(logit[s % 2][:, :, 0:HEADS], u_sum[:], z_ps[s % 2][:, :, D_MSG:ROW],
                                            ALU.add).then_inc(logit_ready, 1)
                if inside(o, STEPS):
                    dve.wait_ge(weight_ready, o + 1)
                    m = msg[:, o_s % 2, :, 0:MSG].rearrange("p t (h c) -> p t h c", c=HC)
                    nc.vector.tensor_tensor(m[:, :, :, 0:D_HEAD],
                                            xl_g[:, o_s, :, 0:D_MSG].rearrange("p t (h d) -> p t h d", d=D_HEAD),
                                            m[:, :, :, D_HEAD:HC].broadcast_to([P, TILES, HEADS, D_HEAD]), ALU.mult
                                            ).then_inc(msg_ready, 1)
                if inside(k, STEPS):
                    dve.wait_ge(LT_done, k + 1)
                    if inside(k - 1, STEPS):
                        dve.wait_ge(F_done, k)
                    nc.vector.tensor_tensor_scan(run_max, starts[:, s], LT_ps, -BIG, ALU.add, ALU.max
                                                 ).then_inc(scan_done, 1)
                if inside(o, STEPS):
                    w_o = dve.value_load(win_tab[0:1, one(o)], min_val=0, max_val=WINDOWS - 1)
                    dve.wait_ge(shrink_ready, o + 1)
                    if inside(o - 1, STEPS):
                        dve.wait_ge(added, o)
                    a = acc[:, bass.DynSlice(w_o, 1), 0:MSG].rearrange("p a (h c) -> p (a h) c", c=HC)
                    nc.vector.tensor_tensor(a, a, shrink[:, o_s % 2].unsqueeze(2).broadcast_to([P, HEADS, HC]),
                                            ALU.mult).then_inc(scaled, 1)
                if inside(k, STEPS):
                    dve.wait_ge(F_done, k + 1)
                    if inside(k - 1, STEPS):
                        dve.wait_ge(ext_done, k)
                    nc.vector.tensor_tensor(last_max[:], F_ps.rearrange("p (t e) -> p t e", e=EXT),
                                            meta[:, s, 2 * TILES:META].bitcast(FP32).unsqueeze(2).broadcast_to(
                                                [P, TILES, EXT]), ALU.mult).then_inc(last_ready, 1)
                    w = dve.value_load(win_tab[0:1, one(k)], min_val=0, max_val=WINDOWS - 1)
                    dve.wait_ge(ext_done, k + 1)
                    nc.vector.tensor_scalar(absent[:], ext_ps[:, :, HEADS], BIG, -BIG, ALU.mult, ALU.add
                                            ).then_inc(absent_done, 1)
                    dve.wait_ge(absent_done, k + 1)
                    nc.vector.tensor_tensor(tile_max[:], ext_ps[:, :, 0:HEADS],
                                            absent[:].unsqueeze(2).broadcast_to([P, TILES, HEADS]), ALU.add
                                            ).then_inc(tile_done, 1)
                    dve.wait_ge(tile_done, k + 1)
                    nc.vector.tensor_reduce(step_max[:], tile_max[:].rearrange("p t h -> p h t"), AX.X, ALU.max
                                            ).then_inc(step_done, 1)
                    dve.wait_ge(step_done, k + 1)
                    if inside(k - 1, STEPS):
                        dve.wait_ge(max_kept, k)
                    if inside(k - 2, STEPS):
                        dve.wait_ge(M_done, k - 1)
                    nc.vector.tensor_tensor(new_max[:, s % 2], step_max[:], at(node_max, w), ALU.max
                                            ).then_inc(max_ready, 1)
                    dve.wait_ge(max_ready, k + 1)
                    if inside(k - 2, STEPS):
                        dve.wait_ge(shrink_ready, k - 1)
                    nc.vector.tensor_tensor(fall[:, s % 2], at(node_max, w), new_max[:, s % 2], ALU.subtract
                                            ).then_inc(fall_ready, 1)
                    dve.wait_ge(fall_ready, k + 1)
                    nc.vector.tensor_scalar(at(node_max, w), new_max[:, s % 2], 1.0, None, ALU.mult
                                            ).then_inc(max_kept, 1)
                if inside(o, STEPS):
                    dve.wait_ge(agg_done, o + 1)
                    dve.wait_ge(scaled, o + 1)
                    nc.vector.tensor_tensor(at(acc, w_o), at(acc, w_o), U_ps[o_s % 2], ALU.add
                                            ).then_inc(added, 1)
                if inside(k, STEPS):
                    dve.wait_ge(M_done, k + 1)
                    nc.vector.tensor_tensor(above[:], logit[s % 2][:, :, 0:HEADS], M_ps, ALU.subtract
                                            ).then_inc(above_done, 1)
                    dve.wait_ge(above_done, k + 1)
                    if inside(k - 2, STEPS):
                        dve.wait_ge(weight_ready, k - 1)
                    nc.vector.tensor_scalar(centred[:, s % 2], above[:], X_LIMIT, None, ALU.min
                                            ).then_inc(centred_ready, 1)


def finale(nc, banks, x_sb, xl_sb, xr_sb, ident, att_relu, Wc_diag, W_outT, bias_col, acc, node_max, out):
    with ExitStack() as ctx:
        def sb(name, shape, dt=FP32):
            return ctx.enter_context(nc.sbuf_tensor(name, shape, dt))

        def sem(name):
            return ctx.enter_context(nc.semaphore(name))

        deg = sb("deg", [P, FB])
        inv_deg = sb("inv_deg", [P, FB])
        mean = sb("mean", [P, FB, D_RBF])
        meanT = sb("meanT", [D_RBF, FB, P])
        z1 = sb("z1", [P, FB, ROW])
        z2 = sb("z2", [P, FB, ROW])
        loop_sum = sb("loop_sum", [P, FB, HEADS])
        loop_logit = sb("loop_logit", [P, FB, HEADS])
        top = sb("top", [P, FB, HEADS])
        falls = sb("falls", [P, 2, FB, HEADS])
        weights = sb("weights", [P, 2, FB, HEADS])
        total = sb("total", [P, FB, HEADS])
        inv_total = sb("inv_total", [P, FB, HEADS])
        oT = sb("oT", [P, FB, P])
        result = sb("result", [P, 2, FB, D_NODE])

        (deg_done, inv_done, mean_done, meanT_done, meanT_ready, attr_done, z_attr, z_right, z_left, z_att,
         z_sum, logit_done, top_done, falls_done, weights_done, old_scaled, loop_msg, sums_done, total_a,
         total_done, inv_total_done, o_ready, oT_done, oT_ready, y_done, result_ready) = map(sem, (
             "deg_done", "inv_done", "mean_done", "meanT_done", "meanT_ready", "attr_done", "z_attr", "z_right",
             "z_left", "z_att", "z_sum", "logit_done", "top_done", "falls_done", "weights_done",
             "old_scaled", "loop_msg", "sums_done", "total_a", "total_done", "inv_total_done", "o_ready",
             "oT_done", "oT_ready", "y_done", "result_ready"))
        written = [sem(f"written{i}") for i in range(2)]
        block = ctx.enter_context(nc.Block())

        def writes(b, parity):
            return sum(1 for i in range(b) if i % 2 == parity)

        T_ps = banks[:, 0:2].rearrange("p b (w d) -> p (b w) d", d=P)
        Y_ps = banks[:, 4:8].rearrange("p b (w d) -> p (b w) d", d=D_NODE)

        @block.tensor
        def _(pe):
            for b in range(FBATCH):
                pe.wait_ge(mean_done, b + 1)
                if b:
                    pe.wait_ge(result_ready, b)
                for i in range(FB):
                    last = nc.tensor.transpose(T_ps[0:D_RBF, i], mean[:, i], ident[:])
                last.then_inc(meanT_done, 1)
                pe.wait_ge(meanT_ready, b + 1)
                for i in range(FB):
                    last = nc.tensor.matmul(Y_ps[:, i, 0:ROW], meanT[:, i], Wc_diag[0:D_RBF, 0:ROW], start=True, stop=True)
                last.then_inc(attr_done, 1)
                pe.wait_ge(o_ready, b + 1)
                for i in range(FB):
                    last = nc.tensor.transpose(T_ps[:, i], z1[:, i, 0:D_MSG], ident[:])
                last.then_inc(oT_done, 1)
                pe.wait_ge(oT_ready, b + 1)
                for i in range(FB):
                    last = nc.tensor.matmul(Y_ps[:, i], oT[:, i], W_outT[:], start=True, stop=True)
                last.then_inc(y_done, 1)

        @block.scalar
        def _(act):
            for b in range(FBATCH):
                act.wait_ge(meanT_done, b + 1)
                nc.scalar.activation(meanT[:], T_ps[0:D_RBF, 0:FB], ACT.Copy).then_inc(meanT_ready, 1)
                act.wait_ge(falls_done, 2 * b + 2)
                nc.scalar.activation(weights[:], falls[:], ACT.Exp).then_inc(weights_done, 1)
                act.wait_ge(oT_done, b + 1)
                nc.scalar.activation(oT[:], T_ps[:, 0:FB], ACT.Identity, bias=bias_col[:]).then_inc(oT_ready, 1)

        @block.vector
        def _(dve):
            def heads(ap):
                return ap[:, :, 0:D_MSG].rearrange("p w (h d) -> p w h d", h=HEADS)

            def spread(ap):
                return ap.unsqueeze(3).broadcast_to([P, FB, HEADS, D_HEAD])

            for b in range(FBATCH):
                ws = slice(b * FB, (b + 1) * FB)
                sums = acc[:, ws, 0:MSG].rearrange("p w (h c) -> p w h c", c=HC)
                nc.vector.tensor_scalar(deg[:], acc[:, ws, MSG], 1.0, None, ALU.max).then_inc(deg_done, 1)
                dve.wait_ge(deg_done, b + 1)
                nc.vector.reciprocal(inv_deg[:], deg[:]).then_inc(inv_done, 1)
                dve.wait_ge(inv_done, b + 1)
                nc.vector.tensor_tensor(mean[:], acc[:, ws, CNT:AGG],
                                        inv_deg[:].unsqueeze(2).broadcast_to([P, FB, D_RBF]), ALU.mult
                                        ).then_inc(mean_done, 1)
                dve.wait_ge(attr_done, b + 1)
                nc.vector.tensor_tensor(z2[:], Y_ps[:, 0:FB, 0:ROW], xr_sb[:, ws], ALU.add).then_inc(z_right, 1)
                dve.wait_ge(z_right, b + 1)
                nc.vector.tensor_tensor(z1[:], z2[:], xl_sb[:, ws], ALU.add).then_inc(z_left, 1)
                dve.wait_ge(z_left, b + 1)
                nc.vector.scalar_tensor_tensor(out=z2[:, :, 0:D_MSG], in0=z1[:, :, 0:D_MSG], scalar=0.0,
                                               in1=att_relu[:].unsqueeze(1).broadcast_to([P, FB, D_MSG]),
                                               op0=ALU.max, op1=ALU.mult).then_inc(z_att, 1)
                dve.wait_ge(z_att, b + 1)
                nc.vector.tensor_reduce(loop_sum[:], heads(z2), AX.X, ALU.add).then_inc(z_sum, 1)
                dve.wait_ge(z_sum, b + 1)
                nc.vector.tensor_tensor(loop_logit[:], loop_sum[:], z1[:, :, D_MSG:ROW], ALU.add
                                        ).then_inc(logit_done, 1)
                dve.wait_ge(logit_done, b + 1)
                nc.vector.tensor_tensor(top[:], loop_logit[:], node_max[:, ws], ALU.max).then_inc(top_done, 1)
                dve.wait_ge(top_done, b + 1)
                nc.vector.tensor_tensor(falls[:, 0], node_max[:, ws], top[:], ALU.subtract).then_inc(falls_done, 1)
                nc.vector.tensor_tensor(falls[:, 1], loop_logit[:], top[:], ALU.subtract).then_inc(falls_done, 1)
                dve.wait_ge(weights_done, b + 1)
                nc.vector.tensor_tensor(heads(z1), sums[:, :, :, 0:D_HEAD], spread(weights[:, 0]), ALU.mult
                                        ).then_inc(old_scaled, 1)
                nc.vector.tensor_tensor(heads(z2), heads(xl_sb[:, ws]), spread(weights[:, 1]), ALU.mult
                                        ).then_inc(loop_msg, 1)
                nc.vector.tensor_tensor(total[:], sums[:, :, :, D_HEAD], weights[:, 0], ALU.mult).then_inc(total_a, 1)
                dve.wait_ge(total_a, b + 1)
                nc.vector.tensor_tensor(inv_total[:], total[:], weights[:, 1], ALU.add).then_inc(total_done, 1)
                dve.wait_ge(total_done, b + 1)
                nc.vector.reciprocal(total[:], inv_total[:]).then_inc(inv_total_done, 1)
                dve.wait_ge(old_scaled, b + 1)
                dve.wait_ge(loop_msg, b + 1)
                nc.vector.tensor_tensor(heads(z2), heads(z1), heads(z2), ALU.add).then_inc(sums_done, 1)
                dve.wait_ge(sums_done, b + 1)
                dve.wait_ge(inv_total_done, b + 1)
                nc.vector.tensor_tensor(heads(z1), heads(z2), spread(total[:]), ALU.mult).then_inc(o_ready, 1)
                if b >= 2:
                    dve.wait_ge(written[b % 2], 16 * writes(b, b % 2))
                dve.wait_ge(y_done, b + 1)
                nc.vector.tensor_tensor(result[:, b % 2], Y_ps[:, 0:FB], x_sb[:, ws], ALU.add
                                        ).then_inc(result_ready, 1)

        @block.sync
        def _(sp):
            for b in range(FBATCH):
                sp.wait_ge(result_ready, b + 1)
                whole = FB if b < FBATCH - 1 else FB - 1
                r0 = b * FB * P
                sp.dma_start(out[r0:r0 + whole * P, :].rearrange("(w p) d -> p w d", p=P),
                             result[:, b % 2, 0:whole]).then_inc(written[b % 2], 16)
            sp.dma_start(out[N - LAST_ROWS:N, :], result[0:LAST_ROWS, (FBATCH - 1) % 2, FB - 1]
                         ).then_inc(written[(FBATCH - 1) % 2], 16)
            for i in range(2):
                sp.wait_ge(written[i], 16 * (writes(FBATCH, i) + (i == (FBATCH - 1) % 2)))


_INS = ["x", "src", "dst", "edge_attr_32"] + ["L0_gnn_" + n for n in (
    "W_n2m", "W_r2m", "Wl", "bl", "Wr", "br", "We", "att", "bias", "W_m2n")]


def kernel(**inputs):
    import concourse.bacc as bacc
    from concourse.bass_utils import run_bass_kernel_spmd as run

    nc = bacc.Bacc("TRN2", target_bir_lowering=False, num_devices=1)
    arrays, args = {}, []
    for name in _INS:
        a = np.ascontiguousarray(inputs[name])
        arrays[f"in_{name}"] = a
        args.append(nc.dram_tensor(f"in_{name}", a.shape, mybir.dt.from_np(a.dtype), kind="ExternalInput").ap())
    args.append(nc.dram_tensor("out_0", (N, D_NODE), FP32, kind="ExternalOutput").ap())
    gat_kernel(nc, *args)
    return run(nc, [arrays], core_ids=[0]).results[0]["out_0"]
```

```python
from contextlib import ExitStack

import numpy as np

import concourse.bass as bass
from concourse import mybir

FP32, BF16, I32 = mybir.dt.float32, mybir.dt.bfloat16, mybir.dt.int32
ALU, ACT, AX = mybir.AluOpType, mybir.ActivationFunctionType, mybir.AxisListType

P = 128
N, D_NODE, D_MSG, D_RBF, HEADS = 6250, 256, 128, 32, 8
D_HEAD = D_MSG // HEADS
E = 206250
TILES = 4
GROUP = TILES * P
GROUPS = -(-E // GROUP)
OVERLAP = GROUPS * GROUP - E
WINDOWS = -(-N // P)
LAST_ROWS = N - (WINDOWS - 1) * P
STEPS = GROUPS + WINDOWS - 1
CHUNKS = -(-GROUPS // P)
ROW = D_MSG + HEADS
PARTS = 3
HC = D_HEAD + 1
MSG = HEADS * HC
CNT = MSG + 1
AGG = CNT + D_RBF
MAXIMA = TILES * HEADS
FILLED = 72
BIG = 2.0 ** 100
NO_NODE = 1 << 20
X_LIMIT = 60.0
EPS = 1e-5
SLOPE = 0.2
RING = 8
UNROLL = 8
META = 3 * TILES
XCHUNKS = 6
WRING = 4
FB = 7
FBATCH = WINDOWS // FB
assert FB * FBATCH == WINDOWS



def sweep(eng, start, lo, hi, end, unroll=UNROLL):
    rounds = (hi - lo) // unroll
    for k in range(start, lo):
        yield k, k % unroll, k // unroll
    with eng.Fori(0, rounds) as b:
        for i in range(lo, lo + unroll):
            yield b * unroll + i, i % unroll, b + i // unroll
    for k in range(lo + rounds * unroll, end):
        yield k, k % unroll, k // unroll


def inside(j, count):
    return not isinstance(j, int) or 0 <= j < count


def one(k):
    return slice(k, k + 1) if isinstance(k, int) else bass.DynSlice(k, 1)


def parts_of(parts, w, i):
    return parts[:, one(w), i].rearrange("p a d -> p (a d)")


def settled(eng, value):
    return value if isinstance(value, int) else eng.snap(eng.to_reg(value))


def high(words):
    return words.bitcast(BF16).rearrange("p (c two) -> p c two", two=2)[:, :, 1]


def at(tile, w):
    if isinstance(w, int):
        return tile[:, w]
    return tile[:, bass.DynSlice(w, 1), :].rearrange("p a d -> p (a d)")



def gat_kernel(nc, x, src, dst, edge_attr, W_n2m, W_r2m, Wl, bl, Wr, br, We, att, bias, W_m2n, out):
    xl_table = nc.dram_tensor("xl_table", (WINDOWS * P, ROW), FP32, kind="Internal").ap()
    xr_table = nc.dram_tensor("xr_table", (WINDOWS * P, ROW), FP32, kind="Internal").ap()
    meta_dram = nc.dram_tensor("meta_dram", (GROUPS, P, META), I32, kind="Internal").ap()
    starts_dram = nc.dram_tensor("starts_dram", (GROUPS, TILES, P), FP32, kind="Internal").ap()

    with ExitStack() as ctx:
        def sb(name, shape, dt=FP32):
            return ctx.enter_context(nc.sbuf_tensor(name, shape, dt))

        xr_parts = sb("xr_parts", [P, WINDOWS, PARTS, ROW], BF16)
        ident = sb("ident", [P, P])
        ident16 = sb("ident16", [P, P], BF16)
        iota_n = sb("iota_n", [P, P])
        att_relu = sb("att_relu", [P, D_MSG])
        Wc_diag = sb("Wc_diag", [P, TILES * ROW])
        W_outT = sb("W_outT", [P, D_NODE])
        bias_col = sb("bias_col", [P, 1])
        base_tab = sb("base_tab", [P, STEPS])
        win_tab = sb("win_tab", [1, STEPS], I32)
        grp_tab = sb("grp_tab", [1, STEPS], I32)
        edge_tab = sb("edge_tab", [1, STEPS], I32)

        banks = ctx.enter_context(nc.psum_tensor("banks", [P, 8, 512], FP32))

        prologue(nc, banks, xl_table, meta_dram, starts_dram,
                 (x, src, dst, W_n2m, W_r2m, Wl, bl, Wr, br, We, att, bias, W_m2n),
                 xr_table, xr_parts, ident, ident16, iota_n, att_relu, Wc_diag, W_outT, bias_col,
                 base_tab, win_tab, grp_tab, edge_tab)

        acc = sb("acc", [P, WINDOWS, AGG])
        node_max = sb("node_max", [P, WINDOWS, HEADS])
        edge_loop(nc, banks, xl_table, meta_dram, starts_dram, edge_attr,
                  xr_parts, ident, ident16, iota_n, att_relu, Wc_diag, base_tab, win_tab, grp_tab, edge_tab,
                  acc, node_max)
        finale(nc, banks, x, xl_table, xr_table, ident, att_relu, Wc_diag, W_outT, bias_col,
               acc, node_max, out)


def prologue(nc, banks, xl_table, meta_dram, starts_dram, inputs,
             xr_table, xr_parts, ident, ident16, iota_n, att_relu, Wc_diag, W_outT, bias_col,
             base_tab, win_tab, grp_tab, edge_tab):
    x, src, dst, W_n2m, W_r2m, Wl, bl, Wr, br, We, att, bias, W_m2n = inputs
    full_w = WINDOWS - 1
    xc = full_w // XCHUNKS
    full_g = GROUPS - 1
    with ExitStack() as ctx:
        def sb(name, shape, dt=FP32):
            return ctx.enter_context(nc.sbuf_tensor(name, shape, dt))

        def sem(name):
            return ctx.enter_context(nc.semaphore(name))

        x_sb = sb("x_sb", [P, WINDOWS, D_NODE])
        lr_sb = sb("lr_sb", [P, WRING, 2 * ROW])
        lr_bias = sb("lr_bias", [P, 2 * ROW])
        rest = sb("rest", [P, WRING, ROW])
        src_i = sb("src_i", [P, CHUNKS, GROUP], I32)
        dst_i = sb("dst_i", [P, CHUNKS, GROUP], I32)
        meta_b = sb("meta_b", [P, 2, P, META], I32)
        starts_b = sb("starts_b", [P, 2, TILES, P])
        masked = sb("masked", [1, OVERLAP], I32)
        lasts_i = sb("lasts_i", [1, GROUPS], I32)
        lasts = sb("lasts", [1, GROUPS])
        below = sb("below", [WINDOWS, GROUPS])
        count = sb("count", [WINDOWS, 1])
        first = sb("first", [WINDOWS, 1])
        first_step = sb("first_step", [WINDOWS, 1])
        begun = sb("begun", [WINDOWS, STEPS])
        walk = sb("walk", [1, 2, STEPS])
        ones = sb("ones", [P, P])
        iota_ni = sb("iota_ni", [P, P], I32)
        iota_si = sb("iota_si", [WINDOWS, STEPS], I32)
        iota_s = sb("iota_s", [WINDOWS, STEPS])
        iota_wi = sb("iota_wi", [P, 1], I32)
        iota_w = sb("iota_w", [P, 1])
        bound_w = sb("bound_w", [P, 1])
        W1 = sb("W1", [P, D_NODE])
        Wr2m = sb("Wr2m", [P, TILES, D_RBF])
        Wlre = sb("Wlre", [P, 3, D_MSG])
        WlreT = sb("WlreT", [P, 3, D_MSG])
        Wout = sb("Wout", [P, 2, D_MSG])
        Wall = sb("Wall", [P, 7, ROW])
        att_bc = sb("att_bc", [P, D_MSG])
        Watt = sb("Watt", [P, 7, D_MSG])
        Wshare = sb("Wshare", [P, 7, HEADS])
        lr_row = sb("lr_row", [1, 2 * D_MSG])
        att_row = sb("att_row", [1, D_MSG])
        bn = sb("bn", [P, WINDOWS, 6])
        mv = sb("mv", [P, WINDOWS, 2])
        var_eps = sb("var_eps", [P, WINDOWS])
        std = sb("std", [P, WINDOWS])
        rstd = sb("rstd", [P, WINDOWS])
        shift = sb("shift", [P, WINDOWS])
        h = sb("h", [P, 2, D_NODE])
        hT = sb("hT", [P, 2, D_NODE])

        x_in = [sem(f"x_in{i}") for i in range(XCHUNKS + 1)]
        flags_out = [sem(f"flags_out{i}") for i in (0, 1)]
        lr_out = [sem(f"lr_out{i}") for i in range(WRING)]
        weights_in, groups_in, lasts_in = map(sem, ("weights_in", "groups_in", "lasts_in"))
        ones_ready, ident_zero, ident_ready, iotas_int, iotas_ready, mask_ready, x_tail_zero, diag_zero = map(
            sem, ("ones_ready", "ident_zero", "ident_ready", "iotas_int", "iotas_ready", "mask_ready",
                  "x_tail_zero", "diag_zero"))
        ident16_ready, bias_spread, bias_ready = map(sem, ("ident16_ready", "bias_spread", "bias_ready"))
        wT_done, wT_ready, w_prod, w_copied, w_att, w_sum, w_share, w_ready = map(
            sem, ("wT_done", "wT_ready", "w_prod", "w_copied", "w_att", "w_sum", "w_share", "w_ready"))
        meta_ready, runs_ready, starts_ready, flags_ready = map(
            sem, ("meta_ready", "runs_ready", "starts_ready", "flags_ready"))
        lasts_ready, lasts_spread, counted, clipped, first_ready, begun_ready, walk_spread, walk_done, grp_done, \
            tabs_ready = map(sem, ("lasts_ready", "lasts_spread", "counted", "clipped", "first_ready",
                                   "begun_ready", "walk_spread", "walk_done", "grp_done", "tabs_ready"))
        bn_done, mv_done, var_done, std_done, rstd_done, shift_done = map(
            sem, ("bn_done", "mv_done", "var_done", "std_done", "rstd_done", "shift_done"))
        h_ready, hT_done, hT_ready, proj_done, lr_ready, hi_ready, rest_ready, mid_ready, lo_ready = map(
            sem, ("h_ready", "hT_done", "hT_ready", "proj_done", "lr_ready", "hi_ready", "rest_ready",
                  "mid_ready", "lo_ready"))
        block = ctx.enter_context(nc.Block())

        hT_ps, proj_ps = [banks[:, i] for i in (0, 1)], [banks[:, i] for i in (2, 3)]
        wps, cps = [banks[:, i] for i in (4, 5)], banks[:, 6]
        n_weights = 5 + TILES + 4

        @block.sync
        def _(sp):
            xw = x[0:full_w * P, :].rearrange("(w p) d -> p w d", p=P)
            for c in range(XCHUNKS):
                sp.dma_start(x_sb[:, c * xc:(c + 1) * xc, :], xw[:, c * xc:(c + 1) * xc, :]).then_inc(x_in[c], 16)
            sp.wait_ge(x_tail_zero, 1)
            sp.dma_start(x_sb[0:LAST_ROWS, full_w, :], x[full_w * P:N, :]).then_inc(x_in[XCHUNKS], 16)
            for c in range(CHUNKS):
                r = min(P, GROUPS - c * P)
                sp.wait_ge(flags_ready, c + 1)
                sp.dma_start(meta_dram[c * P:c * P + r], meta_b[0:r, c % 2]).then_inc(flags_out[c % 2], 16)
                sp.dma_start(starts_dram[c * P:c * P + r], starts_b[0:r, c % 2]).then_inc(flags_out[c % 2], 16)
            for w, s, _ in sweep(sp, 0, WRING, WINDOWS, WINDOWS, WRING):
                sp.wait_ge(lr_ready, w + 1)
                sp.dma_start(xl_table[bass.DynSlice(w * P, P), :], lr_sb[:, s, 0:ROW]).then_inc(lr_out[s], 16)
                sp.dma_start(xr_table[bass.DynSlice(w * P, P), :], lr_sb[:, s, ROW:]).then_inc(lr_out[s], 16)
            for i in (0, 1):
                sp.wait_ge(flags_out[i], 32 * (CHUNKS // 2))
            for s in range(WRING):
                sp.wait_ge(lr_out[s], 32 * (-(-(WINDOWS - s) // WRING)))

        @block.gpsimd
        def _(pool):
            nc.gpsimd.memset(ones[:], 1.0).then_inc(ones_ready, 1)
            nc.gpsimd.memset(ident[:], 0.0).then_inc(ident_zero, 1)
            nc.gpsimd.memset(x_sb[:, full_w, :], 0.0).then_inc(x_tail_zero, 1)
            nc.gpsimd.memset(masked[:], NO_NODE).then_inc(mask_ready, 1)
            nc.gpsimd.iota(iota_ni[:], pattern=[[1, P]], base=0, channel_multiplier=0).then_inc(iotas_int, 1)
            nc.gpsimd.iota(iota_si[:], pattern=[[1, STEPS]], base=0, channel_multiplier=0).then_inc(iotas_int, 1)
            nc.gpsimd.iota(iota_wi[:], pattern=[[0, 1]], base=0, channel_multiplier=1).then_inc(iotas_int, 1)
            pool.wait_ge(ident_zero, 1)
            nc.gpsimd.affine_select(out=ident[:], in_=ident[:], compare_op=ALU.not_equal, fill=1.0, base=0,
                                    pattern=[[-1, P]], channel_multiplier=1).then_inc(ident_ready, 1)
            nc.gpsimd.memset(Wc_diag[:], 0.0).then_inc(diag_zero, 1)
            pool.wait_ge(ident_ready, 1)
            nc.gpsimd.tensor_copy(ident16[:], ident[:]).then_inc(ident16_ready, 1)

        @block.scalar
        def _(act):
            for c in range(CHUNKS):
                r = min(P, full_g - c * P)
                for to, of in ((src_i, src), (dst_i, dst)):
                    act.dma_start(to[0:r, c], of[c * P * GROUP:(c * P + r) * GROUP].rearrange("(g k) -> g k", k=GROUP)
                                  ).then_inc(groups_in, 16)
            tail = full_g - (CHUNKS - 1) * P
            act.dma_start(src_i[tail:tail + 1, CHUNKS - 1], src[E - GROUP:E].rearrange("(a k) -> a k", a=1)
                          ).then_inc(groups_in, 16)
            act.dma_start(dst_i[tail:tail + 1, CHUNKS - 1, OVERLAP:], dst[E - GROUP + OVERLAP:E].rearrange(
                "(a k) -> a k", a=1)).then_inc(groups_in, 16)
            act.wait_ge(mask_ready, 1)
            act.dma_start(dst_i[tail:tail + 1, CHUNKS - 1, 0:OVERLAP], masked[:]).then_inc(groups_in, 16)
            act.dma_start(lasts_i[0:1, 0:full_g], dst[0:full_g * GROUP].rearrange("(g k) -> k g", k=GROUP)[
                GROUP - 1:GROUP, :], allow_slow_non_contiguous=True).then_inc(lasts_in, 16)
            act.dma_start(lasts_i[0:1, full_g:GROUPS], dst[E - 1:E].rearrange("(a k) -> a k", a=1)
                          ).then_inc(lasts_in, 16)
            act.dma_start(W1[:], W_n2m).then_inc(weights_in, 16)
            for i, w in enumerate((Wl, Wr, We)):
                act.dma_start(Wlre[:, i], w).then_inc(weights_in, 16)
            for t in range(TILES):
                act.dma_start(Wr2m[:, t], W_r2m).then_inc(weights_in, 16)
            act.dma_start(Wout[:], W_m2n.rearrange("(c p) m -> p c m", p=P)).then_inc(weights_in, 16)
            act.dma_start(lr_row[0:1, 0:D_MSG], bl.rearrange("(a k) -> a k", a=1)).then_inc(weights_in, 16)
            act.dma_start(lr_row[0:1, D_MSG:], br.rearrange("(a k) -> a k", a=1)).then_inc(weights_in, 16)
            act.dma_start(att_row[0:1, :].rearrange("a (h d) -> a h d", h=HEADS),
                          att.rearrange("(a h) d -> a h d", a=1)).then_inc(weights_in, 16)
            act.dma_start(bias_col[:], bias.rearrange("(p a) -> p a", a=1)).then_inc(weights_in, 16)
            act.wait_ge(var_done, 1)
            nc.scalar.activation(std[:], var_eps[:], ACT.Sqrt).then_inc(std_done, 1)

            act.wait_ge(shift_done, 1)

            for w, s, _ in sweep(act, -2, WRING, WINDOWS - 2, WINDOWS + 2, WRING):
                if inside(w + 2, WINDOWS):
                    if inside(w, WINDOWS):
                        act.wait_ge(hT_done, w + 1)
                    nc.scalar.activation(h[:, s % 2], at(x_sb, w + 2), ACT.Relu, bias=shift[:, one(w + 2)],
                                         scale=rstd[:, one(w + 2)]).then_inc(h_ready, 1)
                if inside(w - 1, WINDOWS):
                    act.wait_ge(lr_ready, w)
                    nc.scalar.activation(parts_of(xr_parts, w - 1, 0), lr_sb[:, (s - 1) % WRING, ROW:], ACT.Copy
                                         ).then_inc(hi_ready, 1)
                if inside(w - 2, WINDOWS):
                    act.wait_ge(rest_ready, w - 1)
                    nc.scalar.activation(parts_of(xr_parts, w - 2, 1), rest[:, (s - 2) % WRING], ACT.Copy
                                         ).then_inc(mid_ready, 1)

        @block.tensor
        def _(pe):
            pe.wait_ge(ident_ready, 1)
            pe.wait_ge(weights_in, 16 * n_weights)
            pe.wait_ge(ones_ready, 1)
            for i in range(3):
                nc.tensor.transpose(wps[0][:, i * P:(i + 1) * P], Wlre[:, i], ident[:]).then_inc(wT_done, 1)
            for i in range(2):
                nc.tensor.transpose(wps[1][:, i * P:(i + 1) * P], Wout[:, i], ident[:]).then_inc(wT_done, 1)
            pe.wait_ge(lasts_ready, 1)
            nc.tensor.matmul(cps[0:WINDOWS, 0:GROUPS], ones[0:1, 0:WINDOWS], lasts[:], start=True, stop=True
                             ).then_inc(lasts_spread, 1)
            pe.wait_ge(wT_ready, 2)
            for c in range(2):
                for i in range(2):
                    nc.tensor.matmul(wps[0][:, (2 * c + i) * P:(2 * c + i + 1) * P], W1[:, c * P:(c + 1) * P],
                                     WlreT[:, i], start=True, stop=True).then_inc(w_prod, 1)
            nc.tensor.matmul(wps[1][:, 0:D_MSG], Wr2m[:].rearrange("p t k -> p (t k)"), WlreT[:, 2],
                             start=True, stop=True).then_inc(w_prod, 1)
            nc.tensor.matmul(wps[1][:, D_MSG:2 * D_MSG], ones[0:1, :], att_row[:], start=True, stop=True
                             ).then_inc(w_prod, 1)
            pe.wait_ge(begun_ready, 1)
            nc.tensor.matmul(cps[:, 0:STEPS], ones[0:WINDOWS, :], begun[:], start=True, stop=True
                             ).then_inc(walk_spread, 1)
            pe.wait_ge(w_share, 1)
            w_of = Wall[:].rearrange("p b r -> p (b r)")
            nc.tensor.matmul(wps[1][:, 0:2 * ROW], ones[0:1, :], w_of[0:1, 4 * ROW:6 * ROW], start=True, stop=True
                             ).then_inc(bias_spread, 1)
            for w, s, _ in sweep(pe, -1, WRING, WINDOWS - 2, WINDOWS, WRING):
                if inside(w + 1, WINDOWS):
                    n = (s + 1) % 2
                    pe.wait_ge(h_ready, w + 2)
                    if inside(w - 1, WINDOWS):
                        pe.wait_ge(hT_ready, w)
                    nc.tensor.transpose(hT_ps[n][:, 0:P], h[:, n, 0:P], ident[:])
                    nc.tensor.transpose(hT_ps[n][:, P:2 * P], h[:, n, P:2 * P], ident[:]).then_inc(hT_done, 1)
                if inside(w, WINDOWS):
                    pe.wait_ge(hT_ready, w + 1)
                    if inside(w - 2, WINDOWS):
                        pe.wait_ge(lr_ready, w - 1)
                    lr = proj_ps[s % 2][:, 0:2 * ROW]
                    nc.tensor.matmul(lr, hT[:, s % 2, 0:P], w_of[:, 0:2 * ROW], start=True, stop=False)
                    nc.tensor.matmul(lr, hT[:, s % 2, P:2 * P], w_of[:, 2 * ROW:4 * ROW], start=False, stop=True
                                     ).then_inc(proj_done, 1)

        @block.vector
        def _(dve):
            dve.wait_ge(groups_in, 16 * (2 * CHUNKS + 3))
            for c in range(CHUNKS):
                r = min(P, GROUPS - c * P)
                m = meta_b[0:r, c % 2]
                if c >= 2:
                    dve.wait_ge(flags_out[c % 2], 32 * (c // 2))
                d = m[:, :, TILES:2 * TILES].bitcast(FP32)
                e = m[:, :, 2 * TILES:META].bitcast(FP32)
                nc.vector.tensor_copy(m[:, :, 0:TILES], src_i[0:r, c].rearrange("g (p t) -> g p t", t=TILES)
                                      ).then_inc(meta_ready, 1)
                nc.vector.tensor_copy(d, dst_i[0:r, c].rearrange("g (p t) -> g p t", t=TILES)).then_inc(meta_ready, 1)
                nc.vector.memset(e[:, P - 1, :], BIG).then_inc(meta_ready, 1)
                nc.vector.memset(starts_b[0:r, c % 2, :, 0], 0.0).then_inc(meta_ready, 1)
                dve.wait_ge(meta_ready, 4 * c + 4)
                nc.vector.tensor_tensor(e[:, 0:P - 1, :], d[:, 1:P, :], d[:, 0:P - 1, :], ALU.not_equal
                                        ).then_inc(runs_ready, 1)
                dve.wait_ge(runs_ready, c + 1)
                nc.vector.tensor_scalar(starts_b[0:r, c % 2, :, 1:P].rearrange("g t p -> g p t"), e[:, 0:P - 1, :],
                                        -BIG, None, ALU.mult).then_inc(starts_ready, 1)
                dve.wait_ge(starts_ready, c + 1)
                nc.vector.tensor_scalar(e[:, 0:P - 1, :], e[:, 0:P - 1, :], BIG, None, ALU.mult).then_inc(flags_ready, 1)
            for w in range(WINDOWS):
                if w % xc == 0:
                    dve.wait_ge(x_in[w // xc], 16)
                nc.vector.bn_stats(bn[:, w], x_sb[:, w]).then_inc(bn_done, 1)
                if w:
                    dve.wait_ge(bn_done, w)
                    nc.vector.bn_aggr(mv[:, w - 1], bn[:, w - 1]).then_inc(mv_done, 1)
            dve.wait_ge(bn_done, WINDOWS)
            nc.vector.bn_aggr(mv[:, WINDOWS - 1], bn[:, WINDOWS - 1]).then_inc(mv_done, 1)
            dve.wait_ge(mv_done, WINDOWS)
            nc.vector.tensor_scalar(var_eps[:], mv[:, :, 1], EPS, None, ALU.add).then_inc(var_done, 1)
            dve.wait_ge(iotas_int, 3)
            nc.vector.tensor_copy(iota_n[:], iota_ni[:]).then_inc(iotas_ready, 1)
            nc.vector.tensor_copy(iota_s[:], iota_si[:]).then_inc(iotas_ready, 1)
            nc.vector.tensor_copy(iota_w[:], iota_wi[:]).then_inc(iotas_ready, 1)
            dve.wait_ge(iotas_ready, 3)
            nc.vector.tensor_scalar(bound_w[:], iota_w[:], float(P), None, ALU.mult).then_inc(iotas_ready, 1)
            dve.wait_ge(lasts_in, 32)
            nc.vector.tensor_copy(lasts[:], lasts_i[:]).then_inc(lasts_ready, 1)
            dve.wait_ge(std_done, 1)
            nc.vector.reciprocal(rstd[:], std[:]).then_inc(rstd_done, 1)
            dve.wait_ge(rstd_done, 1)
            nc.vector.scalar_tensor_tensor(out=shift[:], in0=mv[:, :, 0], scalar=-1.0, in1=rstd[:],
                                           op0=ALU.mult, op1=ALU.mult).then_inc(shift_done, 1)
            dve.wait_ge(wT_done, 5)
            nc.vector.tensor_copy(WlreT[:].rearrange("p i d -> p (i d)"), wps[0][:, 0:3 * P]).then_inc(wT_ready, 1)
            nc.vector.tensor_copy(W_outT[:], wps[1][:, 0:2 * P]).then_inc(wT_ready, 1)
            dve.wait_ge(w_prod, 6)
            dve.wait_ge(diag_zero, 1)
            nc.vector.memset(Wall[:, 4:6], 0.0).then_inc(w_copied, 1)
            nc.vector.tensor_copy(Wall[:, 0:4, 0:D_MSG], wps[0][:, 0:4 * P].rearrange("p (b d) -> p b d", b=4)
                                  ).then_inc(w_copied, 1)
            nc.vector.tensor_copy(Wall[:, 6, 0:D_MSG], wps[1][:, 0:D_MSG]).then_inc(w_copied, 1)
            nc.vector.tensor_copy(att_bc[:], wps[1][:, D_MSG:2 * D_MSG]).then_inc(w_copied, 1)
            nc.vector.tensor_scalar(att_relu[:], wps[1][:, D_MSG:2 * D_MSG], 1.0 - SLOPE, None, ALU.mult
                                    ).then_inc(w_copied, 1)
            dve.wait_ge(w_copied, 5)
            nc.vector.tensor_copy(Wall[0:1, 4:6, 0:D_MSG], lr_row[:].rearrange("p (b d) -> p b d", b=2)
                                  ).then_inc(w_copied, 1)
            dve.wait_ge(w_copied, 6)
            nc.vector.tensor_tensor(Watt[:], Wall[:, :, 0:D_MSG], att_bc[:].unsqueeze(1).broadcast_to([P, 7, D_MSG]),
                                    ALU.mult).then_inc(w_att, 1)
            dve.wait_ge(w_att, 1)
            nc.vector.tensor_reduce(Wshare[:], Watt[:].rearrange("p b (h d) -> p b h d", h=HEADS), AX.X, ALU.add
                                    ).then_inc(w_sum, 1)
            dve.wait_ge(w_sum, 1)
            nc.vector.tensor_scalar(Wall[:, :, D_MSG:ROW], Wshare[:], SLOPE, None, ALU.mult).then_inc(w_share, 1)
            dve.wait_ge(w_share, 1)
            for t in range(TILES):
                q = slice(t * D_RBF, (t + 1) * D_RBF)
                nc.vector.tensor_copy(Wc_diag[q, t * ROW:(t + 1) * ROW], Wall[q, 6]).then_inc(w_ready, 1)
            dve.wait_ge(lasts_spread, 1)
            dve.wait_ge(iotas_ready, 4)
            nc.vector.tensor_scalar(below[:], cps[0:WINDOWS, 0:GROUPS], bound_w[0:WINDOWS], None, ALU.is_lt
                                    ).then_inc(counted, 1)
            dve.wait_ge(counted, 1)
            nc.vector.reduce_sum(count[:], below[:], AX.X).then_inc(counted, 1)
            dve.wait_ge(counted, 2)
            nc.vector.tensor_scalar(first[:], count[:], float(GROUPS - 1), None, ALU.min).then_inc(clipped, 1)
            dve.wait_ge(clipped, 1)
            nc.vector.tensor_tensor(first_step[:], first[:], iota_w[0:WINDOWS], ALU.add).then_inc(first_ready, 1)
            dve.wait_ge(first_ready, 1)
            nc.vector.tensor_scalar(begun[:], iota_s[:], first_step[:], None, ALU.is_ge).then_inc(begun_ready, 1)
            dve.wait_ge(walk_spread, 1)
            nc.vector.tensor_scalar(base_tab[:], cps[:, 0:STEPS], -1.0, float(P), ALU.add, ALU.mult).then_inc(tabs_ready, 1)
            nc.vector.tensor_scalar(walk[0:1, 0], cps[0:1, 0:STEPS], -1.0, None, ALU.add).then_inc(walk_done, 1)
            dve.wait_ge(walk_done, 1)
            nc.vector.tensor_copy(win_tab[:], walk[0:1, 0]).then_inc(tabs_ready, 1)
            nc.vector.tensor_tensor(walk[0:1, 1], iota_s[0:1, :], walk[0:1, 0], ALU.subtract).then_inc(grp_done, 1)
            dve.wait_ge(grp_done, 1)
            nc.vector.tensor_copy(grp_tab[:], walk[0:1, 1]).then_inc(tabs_ready, 1)
            nc.vector.tensor_scalar(edge_tab[:], walk[0:1, 1], float(GROUP), float(E - GROUP), ALU.mult, ALU.min
                                    ).then_inc(tabs_ready, 1)
            dve.wait_ge(bias_spread, 1)
            nc.vector.tensor_copy(lr_bias[:], wps[1][:, 0:2 * ROW]).then_inc(bias_ready, 1)
            dve.wait_ge(bias_ready, 1)
            for w, s, r in sweep(dve, -1, WRING, WINDOWS - 2, WINDOWS + 2, WRING):
                if inside(w + 1, WINDOWS):
                    dve.wait_ge(hT_done, w + 2)
                    if inside(w - 1, WINDOWS):
                        dve.wait_ge(proj_done, w)
                    nc.vector.tensor_copy(hT[:, (s + 1) % 2], hT_ps[(s + 1) % 2][:, 0:2 * P]).then_inc(hT_ready, 1)
                if inside(w, WINDOWS):
                    dve.wait_ge(proj_done, w + 1)
                    if inside(w - WRING, WINDOWS):
                        dve.wait_ge(lr_out[s], r * 32)
                        dve.wait_ge(hi_ready, w - WRING + 1)
                    nc.vector.tensor_tensor(lr_sb[:, s], proj_ps[s % 2][:, 0:2 * ROW], lr_bias[:], ALU.add
                                            ).then_inc(lr_ready, 1)
                if inside(w - 1, WINDOWS):
                    dve.wait_ge(hi_ready, w)
                    nc.vector.tensor_tensor(rest[:, (s - 1) % WRING], lr_sb[:, (s - 1) % WRING, ROW:],
                                            parts_of(xr_parts, w - 1, 0), ALU.subtract).then_inc(rest_ready, 1)
                if inside(w - 2, WINDOWS):
                    dve.wait_ge(mid_ready, w - 1)
                    nc.vector.tensor_tensor(parts_of(xr_parts, w - 2, 2), rest[:, (s - 2) % WRING],
                                            parts_of(xr_parts, w - 2, 1), ALU.subtract).then_inc(lo_ready, 1)


def edge_loop(nc, banks, xl_table, meta_dram, starts_dram, edge_attr,
              xr_parts, ident, ident16, iota_n, att_relu, Wc_diag, base_tab, win_tab, grp_tab, edge_tab,
              acc, node_max):
    with ExitStack() as ctx:
        def sb(name, shape, dt=FP32):
            return ctx.enter_context(nc.sbuf_tensor(name, shape, dt))

        def sem(name):
            return ctx.enter_context(nc.semaphore(name))

        meta = sb("meta", [P, RING, META], I32)
        rbf = sb("rbf", [P, RING, TILES * D_RBF])
        starts = sb("starts", [MAXIMA, RING, P])
        xl_g = sb("xl_g", [P, RING, TILES, ROW])
        minus_slot = sb("minus_slot", [P, TILES])
        distance = sb("distance", [P, TILES, P])
        onehot = sb("onehot", [P, RING, TILES, P])
        onehotT = sb("onehotT", [P, 4, GROUP], BF16)
        rbfT = sb("rbfT", [P, 2, P])
        z = sb("z", [P, 2, TILES, ROW])
        u_att = sb("u_att", [P, TILES, D_MSG])
        u_sum = sb("u_sum", [P, TILES, HEADS])
        logit_all = sb("logit_all", [P, 2, FILLED])
        logit = [logit_all[:, i, 0:MAXIMA].rearrange("p (t h) -> p t h", h=HEADS) for i in (0, 1)]
        run_all = sb("run_all", [FILLED, P])
        run_max = run_all[0:MAXIMA, :]
        last_max = sb("last_max", [P, TILES, HEADS])
        last_lo = sb("last_lo", [P, TILES, HEADS], BF16)
        minus_big = sb("minus_big", [P, MAXIMA], BF16)
        step_max = sb("step_max", [P, HEADS])
        new_max = sb("new_max", [P, HEADS])
        max_lo = sb("max_lo", [P, HEADS], BF16)
        fall = sb("fall", [P, 2, HEADS])
        shrink = sb("shrink", [P, 2, HEADS])
        above = sb("above", [P, TILES, HEADS])
        centred = sb("centred", [P, TILES, HEADS])
        msg = sb("msg", [P, 2, TILES, AGG])

        z_ps = banks[:, 0:2].rearrange("p b (t d) -> p (b t) d", t=2)
        ohT_ps = banks[:, 2, 0:GROUP // 2].bitcast(BF16)
        rbfT_ps = banks[:, 2, GROUP // 2:GROUP // 2 + P]
        LT_all, LT_ps = banks[0:FILLED, 3, 0:P], banks[0:MAXIMA, 3, 0:P]
        FT_all, FT_ps = banks[:, 4, 0:FILLED], banks[:, 4, 0:MAXIMA].rearrange("p (t h) -> p t h", h=HEADS)
        ext_all, ext_ps = banks[:, 5, 0:MAXIMA], banks[:, 5, 0:MAXIMA].rearrange("p (t h) -> p t h", h=HEADS)
        M_ps = banks[:, 6, 0:MAXIMA].rearrange("p (t h) -> p t h", h=HEADS)
        U_ps = banks[:, 7, 0:AGG]

        loads = [sem(f"loads{i}") for i in range(RING)]
        gathers = [sem(f"gathers{i}") for i in range(RING)]
        FULL, GATHERED = 3 * 16, TILES * 16
        state_ready, ones_set = sem("state_ready"), sem("ones_set")
        (slot_ready, dist_ready, oh_ready, ohT_done, ohT_ready, rbfT_ready, z_done, z_ready, att_done, sum_done,
         logit_ready, LT_done, scan_done, FT_done, last_ready, last_lo_ready, ext_done, step_done, max_ready,
         fall_ready, max_kept, max_lo_ready, M_done, above_done, centred_ready, weight_ready, shrink_ready,
         attr_ready, msg_ready, agg_done, scaled, added) = map(sem, (
             "slot_ready", "dist_ready", "oh_ready", "ohT_done", "ohT_ready", "rbfT_ready", "z_done", "z_ready",
             "att_done", "sum_done", "logit_ready", "LT_done", "scan_done", "FT_done", "last_ready", "last_lo_ready",
             "ext_done", "step_done", "max_ready", "fall_ready", "max_kept", "max_lo_ready", "M_done", "above_done",
             "centred_ready", "weight_ready", "shrink_ready", "attr_ready", "msg_ready", "agg_done", "scaled", "added"))
        block = ctx.enter_context(nc.Block())
        first, last_turn = -3, STEPS + 3
        looped = (RING - 3, STEPS - 3)

        @block.sync
        def _(sp):
            for k, s, _ in sweep(sp, 0, RING, STEPS, STEPS):
                if inside(k - RING, STEPS):
                    sp.wait_ge(agg_done, k - RING + 1)
                g = sp.value_load(grp_tab[0:1, one(k)], min_val=0, max_val=GROUPS - 1)
                e = sp.value_load(edge_tab[0:1, one(k)], min_val=0, max_val=E - GROUP)
                sp.dma_start(meta[:, s], meta_dram[bass.DynSlice(g, 1)].rearrange("g p m -> p (g m)")
                             ).then_inc(loads[s], 16)
                sp.dma_start(rbf[:, s], edge_attr[bass.DynSlice(e, GROUP), :].rearrange("(p t) k -> p (t k)", t=TILES)
                             ).then_inc(loads[s], 16)
                row = starts_dram[bass.DynSlice(g, 1)].rearrange("g t p -> t g p")
                sp.dma_start(starts[:, s], row.broadcast_to([TILES, HEADS, P])).then_inc(loads[s], 16)

        @block.gpsimd
        def _(pool):
            nc.gpsimd.memset(logit_all[:], 1.0).then_inc(state_ready, 1)
            nc.gpsimd.memset(run_all[:], 0.0).then_inc(state_ready, 1)
            nc.gpsimd.memset(minus_big[:], -BIG).then_inc(state_ready, 1)
            for k, s, r in sweep(pool, 0, RING, STEPS, STEPS):
                full = settled(pool, (r + 1) * FULL)
                pool.wait_ge(state_ready, 3)
                pool.wait_ge(loads[s], full)
                for t in range(TILES):
                    pool.indirect_dma_start(out=xl_g[:, s, t], out_offset=None, in_=xl_table,
                                            in_offset=bass.IndirectOffsetOnAxis(ap=meta[:, s, t:t + 1], axis=0)
                                            ).then_inc(gathers[s], 16)

        @block.tensor
        def _(pe):
            for k, s, r in sweep(pe, first, *looped, last_turn):
                if inside(k + 1, STEPS):
                    w = pe.value_load(win_tab[0:1, one(k + 1)], min_val=0, max_val=WINDOWS - 1)
                if inside(k - 3, STEPS):
                    pe.wait_ge(msg_ready, k - 2)
                    pe.wait_ge(attr_ready, k - 2)
                    if inside(k - 4, STEPS):
                        pe.wait_ge(added, k - 3)
                    for t in range(TILES):
                        mm = nc.tensor.matmul(U_ps, onehot[:, (s - 3) % RING, t], msg[:, (s - 3) % 2, t],
                                              start=t == 0, stop=t == TILES - 1)
                    mm.then_inc(agg_done, 1)
                if inside(k - 1, STEPS):
                    pe.wait_ge(scan_done, k)
                    nc.tensor.transpose(FT_all, run_all[:], ident[0:FILLED, 0:FILLED]).then_inc(FT_done, 1)
                if inside(k - 2, STEPS):
                    pe.wait_ge(max_lo_ready, k - 1)
                    for t in range(TILES):
                        to_edges = onehotT[:, (s - 2) % 4, t * P:(t + 1) * P]
                        nc.tensor.matmul(M_ps[:, t], to_edges, high(new_max[:]), start=True, stop=False)
                        mm = nc.tensor.matmul(M_ps[:, t], to_edges, max_lo[:], start=False, stop=True)
                    mm.then_inc(M_done, 1)
                if inside(k + 1, STEPS):
                    pe.wait_ge(rbfT_ready, k + 2)
                    if inside(k, STEPS):
                        pe.wait_ge(z_ready, k + 1)
                    for t in range(0, TILES, 2):
                        nc.tensor.matmul(z_ps[:, t:t + 2, 0:ROW], rbfT[:, (s + 1) % 2],
                                         Wc_diag[:, t * ROW:(t + 2) * ROW], start=True, stop=False)
                if inside(k + 2, STEPS):
                    pe.wait_ge(oh_ready, k + 3)
                    if inside(k + 1, STEPS):
                        pe.wait_ge(rbfT_ready, k + 2)
                    for t in range(TILES):
                        nc.tensor.transpose(ohT_ps[:, t * P:(t + 1) * P], high(onehot[:, (s + 2) % RING, t]), ident16[:])
                    nc.tensor.transpose(rbfT_ps, rbf[:, (s + 2) % RING], ident[:]).then_inc(ohT_done, 1)
                if inside(k - 1, STEPS):
                    pe.wait_ge(last_lo_ready, k)
                    nc.tensor.matmul(ext_all, ident16[:], minus_big[:], start=True, stop=False)
                    for t in range(TILES):
                        to_nodes = high(onehot[:, (s - 1) % RING, t])
                        flag = high(meta[:, (s - 1) % RING, 2 * TILES + t:2 * TILES + t + 1])
                        nc.tensor.matmul(ext_ps[:, t], to_nodes, flag.broadcast_to([P, HEADS]), start=False, stop=False)
                        nc.tensor.matmul(ext_ps[:, t], to_nodes, high(last_max[:, t]), start=False, stop=False)
                        mm = nc.tensor.matmul(ext_ps[:, t], to_nodes, last_lo[:, t], start=False, stop=t == TILES - 1)
                    mm.then_inc(ext_done, 1)
                if inside(k, STEPS):
                    full = settled(pe, k + 1)
                    pe.wait_ge(state_ready, 3)
                    pe.wait_ge(logit_ready, full)
                    nc.tensor.transpose(LT_all, logit_all[:, s % 2], ident[:]).then_inc(LT_done, 1)
                if inside(k + 1, STEPS):
                    pe.wait_ge(ohT_ready, k + 2)
                    for t in range(TILES):
                        for part in range(PARTS):
                            mm = nc.tensor.matmul(z_ps[:, t, 0:ROW], onehotT[:, (s + 1) % 4, t * P:(t + 1) * P],
                                                  parts_of(xr_parts, w, part),
                                                  start=False, stop=t % 2 == 1 and part == PARTS - 1)
                    mm.then_inc(z_done, 1)

        @block.scalar
        def _(act):
            for k, s, r in sweep(act, first, *looped, last_turn):
                if inside(k + 3, STEPS):
                    s3, r3 = (s + 3) % RING, r + (s + 3) // RING
                    act.wait_ge(loads[s3], (r3 + 1) * FULL)
                    nc.scalar.activation(minus_slot[:], meta[:, s3, TILES:2 * TILES].bitcast(FP32), ACT.Identity,
                                         scale=-1.0, bias=base_tab[:, one(k + 3)]).then_inc(slot_ready, 1)
                if inside(k - 2, STEPS):
                    if inside(k - 4, STEPS):
                        act.wait_ge(agg_done, k - 3)
                    nc.scalar.activation(msg[:, s % 2, :, CNT:AGG],
                                         rbf[:, (s - 2) % RING].rearrange("p (t k) -> p t k", t=TILES), ACT.Copy
                                         ).then_inc(attr_ready, 1)
                if inside(k + 3, STEPS):
                    act.wait_ge(slot_ready, k + 4)
                    for t in range(TILES):
                        nc.scalar.activation(distance[:, t], iota_n[:], ACT.Abs, bias=minus_slot[:, t:t + 1]
                                             ).then_inc(dist_ready, 1)
                if inside(k - 2, STEPS):
                    act.wait_ge(fall_ready, k - 1)
                    nc.scalar.activation(shrink[:, s % 2], fall[:, s % 2], ACT.Exp).then_inc(shrink_ready, 1)
                if inside(k + 3, STEPS):
                    act.wait_ge(dist_ready, (k + 4) * TILES)
                    nc.scalar.activation(onehot[:, (s + 3) % RING], distance[:], ACT.Relu, scale=-1.0, bias=1.0
                                         ).then_inc(oh_ready, 1)
                if inside(k - 2, STEPS):
                    act.wait_ge(centred_ready, k - 1)
                    nc.scalar.activation(msg[:, s % 2, :, 0:MSG].rearrange("p t (h c) -> p t h c", c=HC)[:, :, :, D_HEAD],
                                         centred[:], ACT.Exp).then_inc(weight_ready, 1)
                if inside(k + 2, STEPS):
                    act.wait_ge(ohT_done, k + 3)
                    nc.scalar.activation(onehotT[:, (s + 2) % 4], ohT_ps, ACT.Copy).then_inc(ohT_ready, 1)
                    nc.scalar.activation(rbfT[:, s % 2], rbfT_ps, ACT.Copy).then_inc(rbfT_ready, 1)

        @block.vector
        def _(dve):
            nc.vector.memset(acc[:], 0.0).then_inc(scaled, 1)
            nc.vector.memset(node_max[:], -BIG).then_inc(max_kept, 1)
            nc.vector.memset(msg[:, :, :, MSG:CNT], 1.0).then_inc(ones_set, 1)
            dve.wait_ge(state_ready, 3)
            dve.wait_ge(ones_set, 1)
            for k, s, r in sweep(dve, first, *looped, last_turn):
                if inside(k - 2, STEPS):
                    w = dve.value_load(win_tab[0:1, one(k - 2)], min_val=0, max_val=WINDOWS - 1)
                if inside(k, STEPS):
                    dve.wait_ge(z_done, k + 1)
                    dve.wait_ge(gathers[s], (r + 1) * GATHERED)
                    nc.vector.tensor_tensor(z[:, s % 2], z_ps[:, :, 0:ROW], xl_g[:, s], ALU.add).then_inc(z_ready, 1)
                if inside(k - 2, STEPS):
                    dve.wait_ge(max_ready, k - 1)
                    nc.vector.tensor_tensor(max_lo[:], new_max[:], high(new_max[:]), ALU.subtract
                                            ).then_inc(max_lo_ready, 1)
                    nc.vector.tensor_tensor(fall[:, s % 2], at(node_max, w), new_max[:], ALU.subtract
                                            ).then_inc(fall_ready, 1)
                if inside(k - 1, STEPS):
                    dve.wait_ge(LT_done, k)
                    nc.vector.tensor_tensor_scan(run_max, starts[:, (s - 1) % RING], LT_ps, -BIG, ALU.add, ALU.max
                                                 ).then_inc(scan_done, 1)
                if inside(k - 2, STEPS):
                    dve.wait_ge(fall_ready, k - 1)
                    nc.vector.tensor_scalar(at(node_max, w), new_max[:], 1.0, None, ALU.mult).then_inc(max_kept, 1)
                if inside(k, STEPS):
                    dve.wait_ge(z_ready, k + 1)
                    nc.vector.scalar_tensor_tensor(out=u_att[:], in0=z[:, s % 2, :, 0:D_MSG], scalar=0.0,
                                                   in1=att_relu[:].unsqueeze(1).broadcast_to([P, TILES, D_MSG]),
                                                   op0=ALU.max, op1=ALU.mult).then_inc(att_done, 1)
                if inside(k - 1, STEPS):
                    dve.wait_ge(FT_done, k)
                    flags = meta[:, (s - 1) % RING, 2 * TILES:META].bitcast(FP32)
                    nc.vector.scalar_tensor_tensor(out=last_max[:], in0=flags.unsqueeze(2).broadcast_to([P, TILES, HEADS]),
                                                   scalar=1.0 / BIG, in1=FT_ps, op0=ALU.mult, op1=ALU.mult
                                                   ).then_inc(last_ready, 1)
                if inside(k - 2, STEPS):
                    dve.wait_ge(M_done, k - 1)
                    nc.vector.tensor_tensor(above[:], logit[s % 2], M_ps, ALU.subtract).then_inc(above_done, 1)
                if inside(k - 1, STEPS):
                    dve.wait_ge(last_ready, k)
                    nc.vector.tensor_tensor(last_lo[:], last_max[:], high(last_max[:].rearrange("p t h -> p (t h)")
                                            ).rearrange("p (t h) -> p t h", h=HEADS), ALU.subtract
                                            ).then_inc(last_lo_ready, 1)
                if inside(k - 2, STEPS):
                    dve.wait_ge(above_done, k - 1)
                    nc.vector.tensor_scalar(centred[:], above[:], X_LIMIT, None, ALU.min).then_inc(centred_ready, 1)
                if inside(k, STEPS):
                    dve.wait_ge(att_done, k + 1)
                    nc.vector.tensor_reduce(u_sum[:], u_att[:].rearrange("p t (h d) -> p t h d", d=D_HEAD),
                                            AX.X, ALU.add).then_inc(sum_done, 1)
                if inside(k - 1, STEPS):
                    w_max = dve.value_load(win_tab[0:1, one(k - 1)], min_val=0, max_val=WINDOWS - 1)
                if inside(k - 3, STEPS):
                    w_sum = dve.value_load(win_tab[0:1, one(k - 3)], min_val=0, max_val=WINDOWS - 1)
                    dve.wait_ge(shrink_ready, k - 2)
                    if inside(k - 4, STEPS):
                        dve.wait_ge(added, k - 3)
                    a = acc[:, one(w_sum), 0:MSG].rearrange("p a (h c) -> p (a h) c", c=HC)
                    nc.vector.tensor_tensor(a, a, shrink[:, (s - 3) % 2].unsqueeze(2).broadcast_to([P, HEADS, HC]),
                                            ALU.mult).then_inc(scaled, 1)
                if inside(k, STEPS):
                    dve.wait_ge(sum_done, k + 1)
                    nc.vector.tensor_tensor(logit[s % 2], u_sum[:], z[:, s % 2, :, D_MSG:ROW], ALU.add
                                            ).then_inc(logit_ready, 1)
                if inside(k - 1, STEPS):
                    dve.wait_ge(ext_done, k)
                    nc.vector.tensor_reduce(step_max[:], ext_ps.rearrange("p t h -> p h t"), AX.X, ALU.max
                                            ).then_inc(step_done, 1)
                if inside(k - 2, STEPS):
                    dve.wait_ge(weight_ready, k - 1)
                    m = msg[:, s % 2, :, 0:MSG].rearrange("p t (h c) -> p t h c", c=HC)
                    nc.vector.tensor_tensor(m[:, :, :, 0:D_HEAD],
                                            xl_g[:, (s - 2) % RING, :, 0:D_MSG].rearrange("p t (h d) -> p t h d", d=D_HEAD),
                                            m[:, :, :, D_HEAD:HC].broadcast_to([P, TILES, HEADS, D_HEAD]), ALU.mult
                                            ).then_inc(msg_ready, 1)
                if inside(k - 1, STEPS):
                    dve.wait_ge(step_done, k)
                    dve.wait_ge(max_kept, k)
                    nc.vector.tensor_tensor(new_max[:], step_max[:], at(node_max, w_max), ALU.max).then_inc(max_ready, 1)
                if inside(k - 3, STEPS):
                    dve.wait_ge(agg_done, k - 2)
                    dve.wait_ge(scaled, k - 1)
                    nc.vector.tensor_tensor(at(acc, w_sum), at(acc, w_sum), U_ps, ALU.add).then_inc(added, 1)


def finale(nc, banks, x, xl_table, xr_table, ident, att_relu, Wc_diag, W_outT, bias_col, acc, node_max, out):
    with ExitStack() as ctx:
        def sb(name, shape, dt=FP32):
            return ctx.enter_context(nc.sbuf_tensor(name, shape, dt))

        def sem(name):
            return ctx.enter_context(nc.semaphore(name))

        x_in = sb("x_in", [P, 2, FB, D_NODE])
        xl_in = sb("xl_in", [P, 2, FB, ROW])
        xr_in = sb("xr_in", [P, 2, FB, ROW])
        deg = sb("deg", [P, FB])
        inv_deg = sb("inv_deg", [P, FB])
        mean = sb("mean", [P, FB, D_RBF])
        meanT = sb("meanT", [D_RBF, FB, P])
        u_att = sb("u_att_loop", [P, FB, D_MSG])
        u_sum = sb("u_sum_loop", [P, FB, HEADS])
        loop_logit = sb("loop_logit", [P, FB, HEADS])
        top = sb("top", [P, FB, HEADS])
        falls = sb("falls", [P, 2, FB, HEADS])
        weights = sb("weights", [P, 2, FB, HEADS])
        old = sb("old", [P, FB, D_MSG])
        own = sb("own", [P, FB, D_MSG])
        both = sb("both", [P, FB, D_MSG])
        gat = sb("gat", [P, FB, D_MSG])
        total_old = sb("total_old", [P, FB, HEADS])
        total = sb("total", [P, FB, HEADS])
        inv_total = sb("inv_total", [P, FB, HEADS])
        gatT = sb("gatT", [P, FB, P])
        result = sb("result", [P, 2, FB, D_NODE])

        (tail_zero, tail_loaded, deg_done, inv_done, mean_done, meanT_done, meanT_ready, z_done, att_done, sum_done, logit_done,
         top_done, falls_done, weights_done, old_done, own_done, both_done, told_done, total_done, itotal_done,
         gat_done, gatT_done, gatT_ready, y_done, result_ready) = map(sem, (
             "tail_zero", "tail_loaded", "deg_done", "inv_done", "mean_done", "meanT_done", "meanT_ready", "zl_done", "attl_done",
             "suml_done", "logitl_done", "top_done", "falls_done", "weights_done", "old_done", "own_done",
             "both_done", "told_done", "total_done", "itotal_done", "gat_done", "gatT_done", "gatT_ready",
             "y_done", "result_ready"))
        loaded = [sem(f"loaded{i}") for i in (0, 1)]
        written = [sem(f"written{i}") for i in (0, 1)]
        block = ctx.enter_context(nc.Block())

        T_ps = banks[:, 0:2].rearrange("p b (w d) -> p (b w) d", d=P)
        z_ps = banks[:, 2:6].rearrange("p b (w d) -> p (b w) d", d=256)
        y_ps = banks[:, 6:8].rearrange("p b (w d) -> p (b w) d", d=D_NODE)
        halves = ((0, 4), (4, FB))
        LOADED = 3 * 16
        turns = (-1, 1, FBATCH - 1, FBATCH, 2)

        def span(tile, b):
            return tile[:, bass.DynSlice(b * FB, FB)]

        @block.sync
        def _(sp):
            def rows(table, b, n=FB):
                return table[bass.DynSlice(b * (FB * P), n * P), :].rearrange("(w p) d -> p w d", p=P)

            def load(b, n=FB):
                s = b % 2
                sp.dma_start(x_in[:, s, 0:n], rows(x, b, n)).then_inc(loaded[s], 16)
                sp.dma_start(xl_in[:, s], rows(xl_table, b)).then_inc(loaded[s], 16)
                sp.dma_start(xr_in[:, s], rows(xr_table, b)).then_inc(loaded[s], 16)

            load(0)
            load(1)
            for b in range(FBATCH):
                sp.wait_ge(result_ready, 2 * (b + 1))
                whole = FB if b < FBATCH - 1 else FB - 1
                sp.dma_start(rows(out, b, whole), result[:, b % 2, 0:whole]).then_inc(written[b % 2], 16)
                if b + 2 < FBATCH - 1:
                    load(b + 2)
                elif b + 2 == FBATCH - 1:
                    sp.wait_ge(tail_zero, 1)
                    load(b + 2, FB - 1)
                    sp.dma_start(x_in[0:LAST_ROWS, b % 2, FB - 1], x[N - LAST_ROWS:N, :]).then_inc(tail_loaded, 16)
            sp.dma_start(out[N - LAST_ROWS:N, :], result[0:LAST_ROWS, (FBATCH - 1) % 2, FB - 1]
                         ).then_inc(written[(FBATCH - 1) % 2], 16)
            for i in (0, 1):
                sp.wait_ge(written[i], 16 * (len(range(i, FBATCH, 2)) + (i == (FBATCH - 1) % 2)))

        @block.gpsimd
        def _(pool):
            pool.wait_ge(result_ready, 2 * (FBATCH - 2))
            nc.gpsimd.memset(x_in[:, (FBATCH - 1) % 2, FB - 1], 0.0).then_inc(tail_zero, 1)

        @block.tensor
        def _(pe):
            for b, s, r in sweep(pe, *turns):
                n, n_s = b + 1, (s + 1) % 2
                n_r = r + (s + 1) // 2
                if inside(n, FBATCH):
                    pe.wait_ge(mean_done, n + 1)
                    if inside(b - 1, FBATCH):
                        pe.wait_ge(gatT_ready, b)
                    for i in range(FB):
                        mm = nc.tensor.transpose(T_ps[0:D_RBF, i], mean[:, i], ident[:])
                    mm.then_inc(meanT_done, 1)
                    pe.wait_ge(loaded[n_s], (n_r + 1) * LOADED)
                    if inside(b, FBATCH):
                        pe.wait_ge(logit_done, n)
                    pe.wait_ge(meanT_ready, n + 1)
                    for i in range(FB):
                        nc.tensor.matmul(z_ps[:, i, 0:ROW], ident[:], xl_in[:, n_s, i], start=True, stop=False)
                        nc.tensor.matmul(z_ps[:, i, 0:ROW], ident[:], xr_in[:, n_s, i], start=False, stop=False)
                        mm = nc.tensor.matmul(z_ps[:, i, 0:ROW], meanT[:, i], Wc_diag[0:D_RBF, 0:ROW],
                                              start=False, stop=True)
                    mm.then_inc(z_done, 1)
                if inside(b, FBATCH):
                    pe.wait_ge(gat_done, b + 1)
                    if isinstance(b, int) and b == FBATCH - 1:
                        pe.wait_ge(tail_loaded, 16)
                    for i in range(FB):
                        mm = nc.tensor.transpose(T_ps[:, i], gat[:, i], ident[:])
                    mm.then_inc(gatT_done, 1)
                    pe.wait_ge(gatT_ready, b + 1)
                    for half, (lo, hi) in enumerate(halves):
                        if half or inside(b - 1, FBATCH):
                            pe.wait_ge(result_ready, b * 2 + half)
                        for i in range(lo, hi):
                            nc.tensor.matmul(y_ps[:, i - lo], gatT[:, i], W_outT[:], start=True, stop=False)
                            mm = nc.tensor.matmul(y_ps[:, i - lo], ident[:], x_in[:, s, i], start=False, stop=True)
                        mm.then_inc(y_done, 1)

        @block.scalar
        def _(act):
            for b, s, r in sweep(act, *turns):
                n = b + 1
                if inside(n, FBATCH):
                    act.wait_ge(meanT_done, n + 1)
                    nc.scalar.activation(meanT[:], T_ps[0:D_RBF, 0:FB], ACT.Copy).then_inc(meanT_ready, 1)
                if inside(b, FBATCH):
                    act.wait_ge(gatT_done, b + 1)
                    nc.scalar.activation(gatT[:], T_ps[:, 0:FB], ACT.Identity, bias=bias_col[:]).then_inc(gatT_ready, 1)
                if inside(n, FBATCH):
                    act.wait_ge(falls_done, n * 2 + 2)
                    nc.scalar.activation(weights[:], falls[:], ACT.Exp).then_inc(weights_done, 1)
                if inside(b, FBATCH):
                    if inside(b - 2, FBATCH):
                        act.wait_ge(written[s], r * 16)
                    for half, (lo, hi) in enumerate(halves):
                        act.wait_ge(y_done, b * 2 + half + 1)
                        nc.scalar.activation(result[:, s, lo:hi], y_ps[:, 0:hi - lo], ACT.Copy
                                             ).then_inc(result_ready, 1)

        @block.vector
        def _(dve):
            def heads(ap):
                return ap.rearrange("p w (h d) -> p w h d", h=HEADS)

            def spread(ap):
                return ap.unsqueeze(3).broadcast_to([P, FB, HEADS, D_HEAD])

            for b, s, r in sweep(dve, *turns):
                n, n_s = b + 1, (s + 1) % 2
                if inside(n, FBATCH):
                    a = span(acc, n)
                    if inside(b, FBATCH):
                        dve.wait_ge(meanT_done, n)
                    nc.vector.tensor_scalar(deg[:], a[:, :, MSG], 1.0, None, ALU.max).then_inc(deg_done, 1)
                    dve.wait_ge(deg_done, n + 1)
                    nc.vector.reciprocal(inv_deg[:], deg[:]).then_inc(inv_done, 1)
                    dve.wait_ge(inv_done, n + 1)
                    nc.vector.tensor_tensor(mean[:], a[:, :, CNT:AGG],
                                            inv_deg[:].unsqueeze(2).broadcast_to([P, FB, D_RBF]), ALU.mult
                                            ).then_inc(mean_done, 1)
                if inside(b, FBATCH):
                    sums = span(acc, b)[:, :, 0:MSG].rearrange("p w (h c) -> p w h c", c=HC)
                    dve.wait_ge(weights_done, b + 1)
                    nc.vector.tensor_tensor(total_old[:], sums[:, :, :, D_HEAD], weights[:, 0], ALU.mult
                                            ).then_inc(told_done, 1)
                    nc.vector.tensor_tensor(heads(old[:]), sums[:, :, :, 0:D_HEAD], spread(weights[:, 0]), ALU.mult
                                            ).then_inc(old_done, 1)
                    dve.wait_ge(told_done, b + 1)
                    nc.vector.tensor_tensor(total[:], total_old[:], weights[:, 1], ALU.add).then_inc(total_done, 1)
                    nc.vector.tensor_tensor(heads(own[:]), heads(xl_in[:, s, :, 0:D_MSG]), spread(weights[:, 1]),
                                            ALU.mult).then_inc(own_done, 1)
                    dve.wait_ge(total_done, b + 1)
                    nc.vector.reciprocal(inv_total[:], total[:]).then_inc(itotal_done, 1)
                    dve.wait_ge(old_done, b + 1)
                    dve.wait_ge(own_done, b + 1)
                    nc.vector.tensor_tensor(both[:], old[:], own[:], ALU.add).then_inc(both_done, 1)
                    dve.wait_ge(both_done, b + 1)
                    dve.wait_ge(itotal_done, b + 1)
                    if inside(b - 1, FBATCH):
                        dve.wait_ge(gatT_done, b)
                    nc.vector.tensor_tensor(heads(gat[:]), heads(both[:]), spread(inv_total[:]), ALU.mult
                                            ).then_inc(gat_done, 1)
                if inside(n, FBATCH):
                    dve.wait_ge(z_done, n + 1)
                    nc.vector.scalar_tensor_tensor(out=u_att[:], in0=z_ps[:, 0:FB, 0:D_MSG], scalar=0.0,
                                                   in1=att_relu[:].unsqueeze(1).broadcast_to([P, FB, D_MSG]),
                                                   op0=ALU.max, op1=ALU.mult).then_inc(att_done, 1)
                    dve.wait_ge(att_done, n + 1)
                    nc.vector.tensor_reduce(u_sum[:], heads(u_att[:]), AX.X, ALU.add).then_inc(sum_done, 1)
                    dve.wait_ge(sum_done, n + 1)
                    nc.vector.tensor_tensor(loop_logit[:], u_sum[:], z_ps[:, 0:FB, D_MSG:ROW], ALU.add
                                            ).then_inc(logit_done, 1)
                    dve.wait_ge(logit_done, n + 1)
                    nc.vector.tensor_tensor(top[:], loop_logit[:], span(node_max, n), ALU.max).then_inc(top_done, 1)
                    dve.wait_ge(top_done, n + 1)
                    nc.vector.tensor_tensor(falls[:, 0], span(node_max, n), top[:], ALU.subtract
                                            ).then_inc(falls_done, 1)
                    nc.vector.tensor_tensor(falls[:, 1], loop_logit[:], top[:], ALU.subtract).then_inc(falls_done, 1)


_INS = ["x", "src", "dst", "edge_attr_32"] + ["L0_gnn_" + n for n in (
    "W_n2m", "W_r2m", "Wl", "bl", "Wr", "br", "We", "att", "bias", "W_m2n")]


def kernel(**inputs):
    import concourse.bacc as bacc
    from concourse.bass_utils import run_bass_kernel_spmd as run

    nc = bacc.Bacc("TRN2", target_bir_lowering=False, num_devices=1)
    arrays, args = {}, []
    for name in _INS:
        a = np.ascontiguousarray(inputs[name])
        arrays[f"in_{name}"] = a
        args.append(nc.dram_tensor(f"in_{name}", a.shape, mybir.dt.from_np(a.dtype), kind="ExternalInput").ap())
    args.append(nc.dram_tensor("out_0", (N, D_NODE), FP32, kind="ExternalOutput").ap())
    gat_kernel(nc, *args)
    return run(nc, [arrays], core_ids=[0]).results[0]["out_0"]
```

```python
from contextlib import ExitStack

import numpy as np

import concourse.bass as bass
from concourse import mybir

FP32, BF16, I32 = mybir.dt.float32, mybir.dt.bfloat16, mybir.dt.int32
ALU, ACT, AX = mybir.AluOpType, mybir.ActivationFunctionType, mybir.AxisListType

P = 128
N, D_NODE, D_MSG, D_RBF, HEADS = 6250, 256, 128, 32, 8
D_HEAD = D_MSG // HEADS
E = 206250
TILES = 4
GROUP = TILES * P
GROUPS = -(-E // GROUP)
OVERLAP = GROUPS * GROUP - E
WINDOWS = -(-N // P)
LAST_ROWS = N - (WINDOWS - 1) * P
STEPS = GROUPS + WINDOWS - 1
CHUNKS = -(-GROUPS // P)
ROW = D_MSG + HEADS
PARTS = 3
HC = D_HEAD + 1
MSG = HEADS * HC
CNT = MSG + 1
AGG = CNT + D_RBF
MAXIMA = TILES * HEADS
FILLED = 72
BIG = 2.0 ** 100
NO_NODE = 1 << 20
EPS = 1e-5
SLOPE = 0.2
RING = 8
UNROLL = 16
META = 3 * TILES
XCHUNKS = 6
WRING = 4
FB = 7
FBATCH = WINDOWS // FB
assert FB * FBATCH == WINDOWS



def sweep(eng, start, lo, hi, end, ring, unroll):
    rounds = (hi - lo) // unroll
    for k in range(start, lo):
        yield k, k % ring, k // ring
    with eng.Fori(0, rounds) as b:
        for i in range(lo, lo + unroll):
            yield b * unroll + i, i % ring, b * (unroll // ring) + i // ring
    for k in range(lo + rounds * unroll, end):
        yield k, k % ring, k // ring


def inside(j, count):
    return not isinstance(j, int) or 0 <= j < count


def one(k):
    return slice(k, k + 1) if isinstance(k, int) else bass.DynSlice(k, 1)


def parts_of(parts, w, i):
    return parts[:, one(w), i].rearrange("p a d -> p (a d)")


def settled(eng, value):
    return value if isinstance(value, int) else eng.snap(eng.to_reg(value))


def high(words):
    return words.bitcast(BF16).rearrange("p (c two) -> p c two", two=2)[:, :, 1]


def at(tile, w):
    if isinstance(w, int):
        return tile[:, w]
    return tile[:, bass.DynSlice(w, 1), :].rearrange("p a d -> p (a d)")



def gat_kernel(nc, x, src, dst, edge_attr, W_n2m, W_r2m, Wl, bl, Wr, br, We, att, bias, W_m2n, out):
    xl_table = nc.dram_tensor("xl_table", (WINDOWS * P, ROW), FP32, kind="Internal").ap()
    both_table = nc.dram_tensor("both_table", (WINDOWS * P, ROW), FP32, kind="Internal").ap()
    meta_dram = nc.dram_tensor("meta_dram", (GROUPS, P, META), I32, kind="Internal").ap()
    starts_dram = nc.dram_tensor("starts_dram", (GROUPS, TILES, P), FP32, kind="Internal").ap()

    with ExitStack() as ctx:
        def sb(name, shape, dt=FP32):
            return ctx.enter_context(nc.sbuf_tensor(name, shape, dt))

        xr_parts = sb("xr_parts", [P, WINDOWS, PARTS, ROW], BF16)
        ident = sb("ident", [P, P])
        ident16 = sb("ident16", [P, P], BF16)
        iota_n = sb("iota_n", [P, P])
        att_relu = sb("att_relu", [P, D_MSG])
        Wc_diag = sb("Wc_diag", [P, TILES * ROW])
        W_outT = sb("W_outT", [P, D_NODE])
        bias_col = sb("bias_col", [P, 1])
        base_tab = sb("base_tab", [P, STEPS])
        win_tab = sb("win_tab", [1, STEPS], I32)
        grp_tab = sb("grp_tab", [1, STEPS], I32)
        edge_tab = sb("edge_tab", [1, STEPS], I32)

        banks = ctx.enter_context(nc.psum_tensor("banks", [P, 8, 512], FP32))

        prologue(nc, banks, xl_table, meta_dram, starts_dram,
                 (x, src, dst, W_n2m, W_r2m, Wl, bl, Wr, br, We, att, bias, W_m2n),
                 both_table, xr_parts, ident, ident16, iota_n, att_relu, Wc_diag, W_outT, bias_col,
                 base_tab, win_tab, grp_tab, edge_tab)

        acc = sb("acc", [P, WINDOWS, AGG])
        node_max = sb("node_max", [P, WINDOWS, HEADS])
        edge_loop(nc, banks, xl_table, meta_dram, starts_dram, edge_attr,
                  xr_parts, ident, ident16, iota_n, att_relu, Wc_diag, base_tab, win_tab, grp_tab, edge_tab,
                  acc, node_max)
        finale(nc, banks, x, xl_table, both_table, ident, att_relu, Wc_diag, W_outT, bias_col,
               acc, node_max, out)


def prologue(nc, banks, xl_table, meta_dram, starts_dram, inputs,
             both_table, xr_parts, ident, ident16, iota_n, att_relu, Wc_diag, W_outT, bias_col,
             base_tab, win_tab, grp_tab, edge_tab):
    x, src, dst, W_n2m, W_r2m, Wl, bl, Wr, br, We, att, bias, W_m2n = inputs
    full_w = WINDOWS - 1
    xc = full_w // XCHUNKS
    full_g = GROUPS - 1
    with ExitStack() as ctx:
        def sb(name, shape, dt=FP32):
            return ctx.enter_context(nc.sbuf_tensor(name, shape, dt))

        def sem(name):
            return ctx.enter_context(nc.semaphore(name))

        x_sb = sb("x_sb", [P, WINDOWS, D_NODE])
        lr_sb = sb("lr_sb", [P, WRING, 2 * ROW])
        lr_bias = sb("lr_bias", [P, 2 * ROW])
        rest = sb("rest", [P, WRING, ROW])
        both = sb("both", [P, WRING, ROW])
        src_i = sb("src_i", [P, CHUNKS, GROUP], I32)
        dst_i = sb("dst_i", [P, CHUNKS, GROUP], I32)
        meta_b = sb("meta_b", [P, 2, P, META], I32)
        starts_b = sb("starts_b", [P, 2, TILES, P])
        masked = sb("masked", [1, OVERLAP], I32)
        lasts_i = sb("lasts_i", [1, GROUPS], I32)
        lasts = sb("lasts", [1, GROUPS])
        below = sb("below", [WINDOWS, GROUPS])
        count = sb("count", [WINDOWS, 1])
        first = sb("first", [WINDOWS, 1])
        first_step = sb("first_step", [WINDOWS, 1])
        begun = sb("begun", [WINDOWS, STEPS])
        walk = sb("walk", [1, 2, STEPS])
        ones = sb("ones", [P, P])
        iota_ni = sb("iota_ni", [P, P], I32)
        iota_si = sb("iota_si", [WINDOWS, STEPS], I32)
        iota_s = sb("iota_s", [WINDOWS, STEPS])
        iota_wi = sb("iota_wi", [P, 1], I32)
        iota_w = sb("iota_w", [P, 1])
        bound_w = sb("bound_w", [P, 1])
        W1 = sb("W1", [P, D_NODE])
        Wr2m = sb("Wr2m", [P, TILES, D_RBF])
        Wlre = sb("Wlre", [P, 3, D_MSG])
        WlreT = sb("WlreT", [P, 3, D_MSG])
        Wout = sb("Wout", [P, 2, D_MSG])
        Wall = sb("Wall", [P, 7, ROW])
        att_bc = sb("att_bc", [P, D_MSG])
        Watt = sb("Watt", [P, 7, D_MSG])
        Wshare = sb("Wshare", [P, 7, HEADS])
        lr_row = sb("lr_row", [1, 2 * D_MSG])
        att_row = sb("att_row", [1, D_MSG])
        bn = sb("bn", [P, WINDOWS, 6])
        mv = sb("mv", [P, WINDOWS, 2])
        var_eps = sb("var_eps", [P, WINDOWS])
        std = sb("std", [P, WINDOWS])
        rstd = sb("rstd", [P, WINDOWS])
        shift = sb("shift", [P, WINDOWS])
        h = sb("h", [P, 2, D_NODE])
        hT = sb("hT", [P, 2, D_NODE])

        x_in = [sem(f"x_in{i}") for i in range(XCHUNKS + 1)]
        flags_out = [sem(f"flags_out{i}") for i in (0, 1)]
        lr_out = [sem(f"lr_out{i}") for i in range(WRING)]
        weights_in, groups_in, lasts_in = map(sem, ("weights_in", "groups_in", "lasts_in"))
        ones_ready, ident_zero, ident_ready, iotas_int, iotas_ready, mask_ready, x_tail_zero, diag_zero = map(
            sem, ("ones_ready", "ident_zero", "ident_ready", "iotas_int", "iotas_ready", "mask_ready",
                  "x_tail_zero", "diag_zero"))
        ident16_ready, bias_spread, bias_ready = map(sem, ("ident16_ready", "bias_spread", "bias_ready"))
        wT_done, wT_ready, w_prod, w_copied, w_att, w_sum, w_share, w_ready = map(
            sem, ("wT_done", "wT_ready", "w_prod", "w_copied", "w_att", "w_sum", "w_share", "w_ready"))
        meta_ready, runs_ready, starts_ready, flags_ready = map(
            sem, ("meta_ready", "runs_ready", "starts_ready", "flags_ready"))
        lasts_ready, lasts_spread, counted, clipped, first_ready, begun_ready, walk_spread, walk_done, grp_done, \
            tabs_ready = map(sem, ("lasts_ready", "lasts_spread", "counted", "clipped", "first_ready",
                                   "begun_ready", "walk_spread", "walk_done", "grp_done", "tabs_ready"))
        bn_done, mv_done, var_done, std_done, rstd_done, shift_done = map(
            sem, ("bn_done", "mv_done", "var_done", "std_done", "rstd_done", "shift_done"))
        h_ready, hT_done, hT_ready, proj_done, lr_ready, both_ready, hi_ready, rest_ready, mid_ready, lo_ready = map(
            sem, ("h_ready", "hT_done", "hT_ready", "proj_done", "lr_ready", "both_ready", "hi_ready", "rest_ready",
                  "mid_ready", "lo_ready"))
        block = ctx.enter_context(nc.Block())

        hT_ps, proj_ps = [banks[:, i] for i in (0, 1)], [banks[:, i] for i in (2, 3)]
        wps, cps = [banks[:, i] for i in (4, 5)], banks[:, 6]
        n_weights = 5 + TILES + 4

        @block.sync
        def _(sp):
            xw = x[0:full_w * P, :].rearrange("(w p) d -> p w d", p=P)
            for c in range(XCHUNKS):
                sp.dma_start(x_sb[:, c * xc:(c + 1) * xc, :], xw[:, c * xc:(c + 1) * xc, :]).then_inc(x_in[c], 16)
            sp.wait_ge(x_tail_zero, 1)
            sp.dma_start(x_sb[0:LAST_ROWS, full_w, :], x[full_w * P:N, :]).then_inc(x_in[XCHUNKS], 16)
            for c in range(CHUNKS):
                r = min(P, GROUPS - c * P)
                sp.wait_ge(flags_ready, c + 1)
                sp.dma_start(meta_dram[c * P:c * P + r], meta_b[0:r, c % 2]).then_inc(flags_out[c % 2], 16)
                sp.dma_start(starts_dram[c * P:c * P + r], starts_b[0:r, c % 2]).then_inc(flags_out[c % 2], 16)
            for w, s, _ in sweep(sp, 0, WRING, WINDOWS, WINDOWS, WRING, WRING):
                sp.wait_ge(lr_ready, w + 1)
                sp.dma_start(xl_table[bass.DynSlice(w * P, P), :], lr_sb[:, s, 0:ROW]).then_inc(lr_out[s], 16)
                sp.wait_ge(both_ready, w + 1)
                sp.dma_start(both_table[bass.DynSlice(w * P, P), :], both[:, s]).then_inc(lr_out[s], 16)
            for i in (0, 1):
                sp.wait_ge(flags_out[i], 32 * (CHUNKS // 2))
            for s in range(WRING):
                sp.wait_ge(lr_out[s], 32 * (-(-(WINDOWS - s) // WRING)))

        @block.gpsimd
        def _(pool):
            nc.gpsimd.memset(ones[:], 1.0).then_inc(ones_ready, 1)
            nc.gpsimd.memset(ident[:], 0.0).then_inc(ident_zero, 1)
            nc.gpsimd.memset(x_sb[:, full_w, :], 0.0).then_inc(x_tail_zero, 1)
            nc.gpsimd.memset(masked[:], NO_NODE).then_inc(mask_ready, 1)
            nc.gpsimd.iota(iota_ni[:], pattern=[[1, P]], base=0, channel_multiplier=0).then_inc(iotas_int, 1)
            nc.gpsimd.iota(iota_si[:], pattern=[[1, STEPS]], base=0, channel_multiplier=0).then_inc(iotas_int, 1)
            nc.gpsimd.iota(iota_wi[:], pattern=[[0, 1]], base=0, channel_multiplier=1).then_inc(iotas_int, 1)
            pool.wait_ge(ident_zero, 1)
            nc.gpsimd.affine_select(out=ident[:], in_=ident[:], compare_op=ALU.not_equal, fill=1.0, base=0,
                                    pattern=[[-1, P]], channel_multiplier=1).then_inc(ident_ready, 1)
            nc.gpsimd.memset(Wc_diag[:], 0.0).then_inc(diag_zero, 1)
            pool.wait_ge(ident_ready, 1)
            nc.gpsimd.tensor_copy(ident16[:], ident[:]).then_inc(ident16_ready, 1)
            for w, s, r in sweep(pool, 0, WRING, WINDOWS, WINDOWS, WRING, WRING):
                pool.wait_ge(lr_ready, w + 1)
                if inside(w - WRING, WINDOWS):
                    pool.wait_ge(lr_out[s], r * 32)
                nc.gpsimd.tensor_tensor(both[:, s], lr_sb[:, s, 0:ROW], lr_sb[:, s, ROW:], ALU.add
                                        ).then_inc(both_ready, 1)

        @block.scalar
        def _(act):
            for c in range(CHUNKS):
                r = min(P, full_g - c * P)
                for to, of in ((src_i, src), (dst_i, dst)):
                    act.dma_start(to[0:r, c], of[c * P * GROUP:(c * P + r) * GROUP].rearrange("(g k) -> g k", k=GROUP)
                                  ).then_inc(groups_in, 16)
            tail = full_g - (CHUNKS - 1) * P
            act.dma_start(src_i[tail:tail + 1, CHUNKS - 1], src[E - GROUP:E].rearrange("(a k) -> a k", a=1)
                          ).then_inc(groups_in, 16)
            act.dma_start(dst_i[tail:tail + 1, CHUNKS - 1, OVERLAP:], dst[E - GROUP + OVERLAP:E].rearrange(
                "(a k) -> a k", a=1)).then_inc(groups_in, 16)
            act.wait_ge(mask_ready, 1)
            act.dma_start(dst_i[tail:tail + 1, CHUNKS - 1, 0:OVERLAP], masked[:]).then_inc(groups_in, 16)
            act.dma_start(lasts_i[0:1, 0:full_g], dst[0:full_g * GROUP].rearrange("(g k) -> k g", k=GROUP)[
                GROUP - 1:GROUP, :], allow_slow_non_contiguous=True).then_inc(lasts_in, 16)
            act.dma_start(lasts_i[0:1, full_g:GROUPS], dst[E - 1:E].rearrange("(a k) -> a k", a=1)
                          ).then_inc(lasts_in, 16)
            act.dma_start(W1[:], W_n2m).then_inc(weights_in, 16)
            for i, w in enumerate((Wl, Wr, We)):
                act.dma_start(Wlre[:, i], w).then_inc(weights_in, 16)
            for t in range(TILES):
                act.dma_start(Wr2m[:, t], W_r2m).then_inc(weights_in, 16)
            act.dma_start(Wout[:], W_m2n.rearrange("(c p) m -> p c m", p=P)).then_inc(weights_in, 16)
            act.dma_start(lr_row[0:1, 0:D_MSG], bl.rearrange("(a k) -> a k", a=1)).then_inc(weights_in, 16)
            act.dma_start(lr_row[0:1, D_MSG:], br.rearrange("(a k) -> a k", a=1)).then_inc(weights_in, 16)
            act.dma_start(att_row[0:1, :].rearrange("a (h d) -> a h d", h=HEADS),
                          att.rearrange("(a h) d -> a h d", a=1)).then_inc(weights_in, 16)
            act.dma_start(bias_col[:], bias.rearrange("(p a) -> p a", a=1)).then_inc(weights_in, 16)
            act.wait_ge(var_done, 1)
            nc.scalar.activation(std[:], var_eps[:], ACT.Sqrt).then_inc(std_done, 1)

            act.wait_ge(shift_done, 1)

            for w, s, _ in sweep(act, -2, WRING, WINDOWS - 2, WINDOWS + 2, WRING, WRING):
                if inside(w + 2, WINDOWS):
                    if inside(w, WINDOWS):
                        act.wait_ge(hT_done, w + 1)
                    nc.scalar.activation(h[:, s % 2], at(x_sb, w + 2), ACT.Relu, bias=shift[:, one(w + 2)],
                                         scale=rstd[:, one(w + 2)]).then_inc(h_ready, 1)
                if inside(w - 1, WINDOWS):
                    act.wait_ge(lr_ready, w)
                    nc.scalar.activation(parts_of(xr_parts, w - 1, 0), lr_sb[:, (s - 1) % WRING, ROW:], ACT.Copy
                                         ).then_inc(hi_ready, 1)
                if inside(w - 2, WINDOWS):
                    act.wait_ge(rest_ready, w - 1)
                    nc.scalar.activation(parts_of(xr_parts, w - 2, 1), rest[:, (s - 2) % WRING], ACT.Copy
                                         ).then_inc(mid_ready, 1)

        @block.tensor
        def _(pe):
            pe.wait_ge(ident_ready, 1)
            pe.wait_ge(weights_in, 16 * n_weights)
            pe.wait_ge(ones_ready, 1)
            for i in range(3):
                nc.tensor.transpose(wps[0][:, i * P:(i + 1) * P], Wlre[:, i], ident[:]).then_inc(wT_done, 1)
            for i in range(2):
                nc.tensor.transpose(wps[1][:, i * P:(i + 1) * P], Wout[:, i], ident[:]).then_inc(wT_done, 1)
            pe.wait_ge(lasts_ready, 1)
            nc.tensor.matmul(cps[0:WINDOWS, 0:GROUPS], ones[0:1, 0:WINDOWS], lasts[:], start=True, stop=True
                             ).then_inc(lasts_spread, 1)
            pe.wait_ge(wT_ready, 2)
            for c in range(2):
                for i in range(2):
                    nc.tensor.matmul(wps[0][:, (2 * c + i) * P:(2 * c + i + 1) * P], W1[:, c * P:(c + 1) * P],
                                     WlreT[:, i], start=True, stop=True).then_inc(w_prod, 1)
            nc.tensor.matmul(wps[1][:, 0:D_MSG], Wr2m[:].rearrange("p t k -> p (t k)"), WlreT[:, 2],
                             start=True, stop=True).then_inc(w_prod, 1)
            nc.tensor.matmul(wps[1][:, D_MSG:2 * D_MSG], ones[0:1, :], att_row[:], start=True, stop=True
                             ).then_inc(w_prod, 1)
            pe.wait_ge(begun_ready, 1)
            nc.tensor.matmul(cps[:, 0:STEPS], ones[0:WINDOWS, :], begun[:], start=True, stop=True
                             ).then_inc(walk_spread, 1)
            pe.wait_ge(w_share, 1)
            w_of = Wall[:].rearrange("p b r -> p (b r)")
            nc.tensor.matmul(wps[1][:, 0:2 * ROW], ones[0:1, :], w_of[0:1, 4 * ROW:6 * ROW], start=True, stop=True
                             ).then_inc(bias_spread, 1)
            for w, s, _ in sweep(pe, -1, WRING, WINDOWS - 2, WINDOWS, WRING, WRING):
                if inside(w + 1, WINDOWS):
                    n = (s + 1) % 2
                    pe.wait_ge(h_ready, w + 2)
                    if inside(w - 1, WINDOWS):
                        pe.wait_ge(hT_ready, w)
                    nc.tensor.transpose(hT_ps[n][:, 0:P], h[:, n, 0:P], ident[:])
                    nc.tensor.transpose(hT_ps[n][:, P:2 * P], h[:, n, P:2 * P], ident[:]).then_inc(hT_done, 1)
                if inside(w, WINDOWS):
                    pe.wait_ge(hT_ready, w + 1)
                    if inside(w - 2, WINDOWS):
                        pe.wait_ge(lr_ready, w - 1)
                    lr = proj_ps[s % 2][:, 0:2 * ROW]
                    nc.tensor.matmul(lr, hT[:, s % 2, 0:P], w_of[:, 0:2 * ROW], start=True, stop=False)
                    nc.tensor.matmul(lr, hT[:, s % 2, P:2 * P], w_of[:, 2 * ROW:4 * ROW], start=False, stop=True
                                     ).then_inc(proj_done, 1)

        @block.vector
        def _(dve):
            early = (XCHUNKS - 1) * xc

            def stats(windows):
                for w in windows:
                    if w % xc == 0:
                        dve.wait_ge(x_in[w // xc], 16)
                    nc.vector.bn_stats(bn[:, w], x_sb[:, w]).then_inc(bn_done, 1)
                    if w:
                        dve.wait_ge(bn_done, w)
                        nc.vector.bn_aggr(mv[:, w - 1], bn[:, w - 1]).then_inc(mv_done, 1)

            dve.wait_ge(iotas_int, 3)
            nc.vector.tensor_copy(iota_n[:], iota_ni[:]).then_inc(iotas_ready, 1)
            nc.vector.tensor_copy(iota_s[:], iota_si[:]).then_inc(iotas_ready, 1)
            nc.vector.tensor_copy(iota_w[:], iota_wi[:]).then_inc(iotas_ready, 1)
            dve.wait_ge(iotas_ready, 3)
            nc.vector.tensor_scalar(bound_w[:], iota_w[:], float(P), None, ALU.mult).then_inc(iotas_ready, 1)
            stats(range(early))
            dve.wait_ge(groups_in, 16 * (2 * CHUNKS + 3))
            for c in range(CHUNKS):
                r = min(P, GROUPS - c * P)
                m = meta_b[0:r, c % 2]
                if c >= 2:
                    dve.wait_ge(flags_out[c % 2], 32 * (c // 2))
                d = m[:, :, TILES:2 * TILES].bitcast(FP32)
                e = m[:, :, 2 * TILES:META].bitcast(FP32)
                nc.vector.tensor_copy(m[:, :, 0:TILES], src_i[0:r, c].rearrange("g (p t) -> g p t", t=TILES)
                                      ).then_inc(meta_ready, 1)
                nc.vector.tensor_copy(d, dst_i[0:r, c].rearrange("g (p t) -> g p t", t=TILES)).then_inc(meta_ready, 1)
                nc.vector.memset(e[:, P - 1, :], BIG).then_inc(meta_ready, 1)
                nc.vector.memset(starts_b[0:r, c % 2, :, 0], 0.0).then_inc(meta_ready, 1)
                dve.wait_ge(meta_ready, 4 * c + 4)
                nc.vector.tensor_tensor(e[:, 0:P - 1, :], d[:, 1:P, :], d[:, 0:P - 1, :], ALU.not_equal
                                        ).then_inc(runs_ready, 1)
                dve.wait_ge(runs_ready, c + 1)
                nc.vector.tensor_scalar(starts_b[0:r, c % 2, :, 1:P].rearrange("g t p -> g p t"), e[:, 0:P - 1, :],
                                        -BIG, None, ALU.mult).then_inc(starts_ready, 1)
                dve.wait_ge(starts_ready, c + 1)
                nc.vector.tensor_scalar(e[:, 0:P - 1, :], e[:, 0:P - 1, :], BIG, None, ALU.mult).then_inc(flags_ready, 1)
            dve.wait_ge(lasts_in, 32)
            nc.vector.tensor_copy(lasts[:], lasts_i[:]).then_inc(lasts_ready, 1)
            dve.wait_ge(wT_done, 5)
            nc.vector.tensor_copy(WlreT[:].rearrange("p i d -> p (i d)"), wps[0][:, 0:3 * P]).then_inc(wT_ready, 1)
            nc.vector.tensor_copy(W_outT[:], wps[1][:, 0:2 * P]).then_inc(wT_ready, 1)
            stats(range(early, WINDOWS))
            dve.wait_ge(bn_done, WINDOWS)
            nc.vector.bn_aggr(mv[:, WINDOWS - 1], bn[:, WINDOWS - 1]).then_inc(mv_done, 1)
            dve.wait_ge(mv_done, WINDOWS)
            nc.vector.tensor_scalar(var_eps[:], mv[:, :, 1], EPS, None, ALU.add).then_inc(var_done, 1)
            dve.wait_ge(std_done, 1)
            nc.vector.reciprocal(rstd[:], std[:]).then_inc(rstd_done, 1)
            dve.wait_ge(rstd_done, 1)
            nc.vector.scalar_tensor_tensor(out=shift[:], in0=mv[:, :, 0], scalar=-1.0, in1=rstd[:],
                                           op0=ALU.mult, op1=ALU.mult).then_inc(shift_done, 1)
            dve.wait_ge(lasts_spread, 1)
            dve.wait_ge(iotas_ready, 4)
            nc.vector.tensor_scalar(below[:], cps[0:WINDOWS, 0:GROUPS], bound_w[0:WINDOWS], None, ALU.is_lt
                                    ).then_inc(counted, 1)
            dve.wait_ge(counted, 1)
            nc.vector.reduce_sum(count[:], below[:], AX.X).then_inc(counted, 1)
            dve.wait_ge(counted, 2)
            nc.vector.tensor_scalar(first[:], count[:], float(GROUPS - 1), None, ALU.min).then_inc(clipped, 1)
            dve.wait_ge(clipped, 1)
            nc.vector.tensor_tensor(first_step[:], first[:], iota_w[0:WINDOWS], ALU.add).then_inc(first_ready, 1)
            dve.wait_ge(first_ready, 1)
            nc.vector.tensor_scalar(begun[:], iota_s[:], first_step[:], None, ALU.is_ge).then_inc(begun_ready, 1)
            dve.wait_ge(w_prod, 6)
            dve.wait_ge(diag_zero, 1)
            nc.vector.memset(Wall[:, 4:6], 0.0).then_inc(w_copied, 1)
            nc.vector.tensor_copy(Wall[:, 0:4, 0:D_MSG], wps[0][:, 0:4 * P].rearrange("p (b d) -> p b d", b=4)
                                  ).then_inc(w_copied, 1)
            nc.vector.tensor_copy(Wall[:, 6, 0:D_MSG], wps[1][:, 0:D_MSG]).then_inc(w_copied, 1)
            nc.vector.tensor_copy(att_bc[:], wps[1][:, D_MSG:2 * D_MSG]).then_inc(w_copied, 1)
            nc.vector.tensor_scalar(att_relu[:], wps[1][:, D_MSG:2 * D_MSG], 1.0 - SLOPE, None, ALU.mult
                                    ).then_inc(w_copied, 1)
            dve.wait_ge(w_copied, 5)
            nc.vector.tensor_copy(Wall[0:1, 4:6, 0:D_MSG], lr_row[:].rearrange("p (b d) -> p b d", b=2)
                                  ).then_inc(w_copied, 1)
            dve.wait_ge(w_copied, 6)
            nc.vector.tensor_tensor(Watt[:], Wall[:, :, 0:D_MSG], att_bc[:].unsqueeze(1).broadcast_to([P, 7, D_MSG]),
                                    ALU.mult).then_inc(w_att, 1)
            dve.wait_ge(w_att, 1)
            nc.vector.tensor_reduce(Wshare[:], Watt[:].rearrange("p b (h d) -> p b h d", h=HEADS), AX.X, ALU.add
                                    ).then_inc(w_sum, 1)
            dve.wait_ge(w_sum, 1)
            nc.vector.tensor_scalar(Wall[:, :, D_MSG:ROW], Wshare[:], SLOPE, None, ALU.mult).then_inc(w_share, 1)
            dve.wait_ge(w_share, 1)
            for t in range(TILES):
                q = slice(t * D_RBF, (t + 1) * D_RBF)
                nc.vector.tensor_copy(Wc_diag[q, t * ROW:(t + 1) * ROW], Wall[q, 6]).then_inc(w_ready, 1)
            dve.wait_ge(walk_spread, 1)
            nc.vector.tensor_scalar(base_tab[:], cps[:, 0:STEPS], -1.0, float(P), ALU.add, ALU.mult).then_inc(tabs_ready, 1)
            nc.vector.tensor_scalar(walk[0:1, 0], cps[0:1, 0:STEPS], -1.0, None, ALU.add).then_inc(walk_done, 1)
            dve.wait_ge(walk_done, 1)
            nc.vector.tensor_copy(win_tab[:], walk[0:1, 0]).then_inc(tabs_ready, 1)
            nc.vector.tensor_tensor(walk[0:1, 1], iota_s[0:1, :], walk[0:1, 0], ALU.subtract).then_inc(grp_done, 1)
            dve.wait_ge(grp_done, 1)
            nc.vector.tensor_copy(grp_tab[:], walk[0:1, 1]).then_inc(tabs_ready, 1)
            nc.vector.tensor_scalar(edge_tab[:], walk[0:1, 1], float(GROUP), float(E - GROUP), ALU.mult, ALU.min
                                    ).then_inc(tabs_ready, 1)
            dve.wait_ge(bias_spread, 1)
            nc.vector.tensor_copy(lr_bias[:], wps[1][:, 0:2 * ROW]).then_inc(bias_ready, 1)
            dve.wait_ge(bias_ready, 1)
            for w, s, r in sweep(dve, -1, WRING, WINDOWS - 2, WINDOWS + 2, WRING, WRING):
                if inside(w + 1, WINDOWS):
                    dve.wait_ge(hT_done, w + 2)
                    if inside(w - 1, WINDOWS):
                        dve.wait_ge(proj_done, w)
                    nc.vector.tensor_copy(hT[:, (s + 1) % 2], hT_ps[(s + 1) % 2][:, 0:2 * P]).then_inc(hT_ready, 1)
                if inside(w, WINDOWS):
                    dve.wait_ge(proj_done, w + 1)
                    if inside(w - WRING, WINDOWS):
                        dve.wait_ge(lr_out[s], r * 32)
                        dve.wait_ge(hi_ready, w - WRING + 1)
                    nc.vector.tensor_tensor(lr_sb[:, s], proj_ps[s % 2][:, 0:2 * ROW], lr_bias[:], ALU.add
                                            ).then_inc(lr_ready, 1)
                if inside(w - 1, WINDOWS):
                    dve.wait_ge(hi_ready, w)
                    nc.vector.tensor_tensor(rest[:, (s - 1) % WRING], lr_sb[:, (s - 1) % WRING, ROW:],
                                            parts_of(xr_parts, w - 1, 0), ALU.subtract).then_inc(rest_ready, 1)
                if inside(w - 2, WINDOWS):
                    dve.wait_ge(mid_ready, w - 1)
                    nc.vector.tensor_tensor(parts_of(xr_parts, w - 2, 2), rest[:, (s - 2) % WRING],
                                            parts_of(xr_parts, w - 2, 1), ALU.subtract).then_inc(lo_ready, 1)


def edge_loop(nc, banks, xl_table, meta_dram, starts_dram, edge_attr,
              xr_parts, ident, ident16, iota_n, att_relu, Wc_diag, base_tab, win_tab, grp_tab, edge_tab,
              acc, node_max):
    with ExitStack() as ctx:
        def sb(name, shape, dt=FP32):
            return ctx.enter_context(nc.sbuf_tensor(name, shape, dt))

        def sem(name):
            return ctx.enter_context(nc.semaphore(name))

        meta = sb("meta", [P, RING, META], I32)
        rbf = sb("rbf", [P, RING, TILES * D_RBF])
        starts = sb("starts", [MAXIMA, RING, P])
        xl_g = sb("xl_g", [P, RING, TILES, ROW])
        minus_slot = sb("minus_slot", [P, TILES])
        distance = sb("distance", [P, TILES, P])
        onehot = sb("onehot", [P, RING, TILES, P])
        onehotT = sb("onehotT", [P, 4, GROUP], BF16)
        rbfT = sb("rbfT", [P, 2, P])
        z = sb("z", [P, 2, TILES, ROW])
        u_att = sb("u_att", [P, TILES, D_MSG])
        u_sum = sb("u_sum", [P, TILES, HEADS])
        logit_all = sb("logit_all", [P, 2, FILLED])
        logit = [logit_all[:, i, 0:MAXIMA].rearrange("p (t h) -> p t h", h=HEADS) for i in (0, 1)]
        run_all = sb("run_all", [FILLED, P])
        run_max = run_all[0:MAXIMA, :]
        last_max = sb("last_max", [P, TILES, HEADS])
        last_lo = sb("last_lo", [P, TILES, HEADS], BF16)
        minus_big = sb("minus_big", [P, MAXIMA], BF16)
        plus_big = sb("plus_big", [P, MAXIMA], BF16)
        step_max = sb("step_max", [P, HEADS])
        new_max = sb("new_max", [P, HEADS])
        max_lo = sb("max_lo", [P, HEADS], BF16)
        fall = sb("fall", [P, 2, HEADS])
        shrink = sb("shrink", [P, 2, HEADS])
        above = sb("above", [P, TILES, HEADS])
        msg = sb("msg", [P, 2, TILES, AGG])

        z_ps = banks[:, 0:2].rearrange("p b (t d) -> p (b t) d", t=2)
        ohT_ps = banks[:, 2, 0:GROUP // 2].bitcast(BF16)
        rbfT_ps = banks[:, 2, GROUP // 2:GROUP // 2 + P]
        LT_all, LT_ps = banks[0:FILLED, 3, 0:P], banks[0:MAXIMA, 3, 0:P]
        FT_all, FT_ps = banks[:, 4, 0:FILLED], banks[:, 4, 0:MAXIMA].rearrange("p (t h) -> p t h", h=HEADS)
        ext_all, ext_ps = banks[:, 5, 0:MAXIMA], banks[:, 5, 0:MAXIMA].rearrange("p (t h) -> p t h", h=HEADS)
        M_all, M_ps = banks[:, 6, 0:MAXIMA], banks[:, 6, 0:MAXIMA].rearrange("p (t h) -> p t h", h=HEADS)
        U_ps = banks[:, 7, 0:AGG]

        loads = [sem(f"loads{i}") for i in range(RING)]
        gathers = [sem(f"gathers{i}") for i in range(RING)]
        FULL, GATHERED = 3 * 16, TILES * 16
        state_ready, ones_set = sem("state_ready"), sem("ones_set")
        (slot_ready, dist_ready, oh_ready, ohT_done, ohT_ready, rbfT_ready, z_done, z_ready, att_done, sum_done,
         logit_ready, LT_done, scan_done, FT_done, last_ready, last_lo_ready, ext_done, step_done, max_ready,
         fall_ready, max_kept, max_lo_ready, M_done, above_ready, weight_ready, shrink_ready,
         attr_ready, msg_ready, agg_done, scaled, added) = map(sem, (
             "slot_ready", "dist_ready", "oh_ready", "ohT_done", "ohT_ready", "rbfT_ready", "z_done", "z_ready",
             "att_done", "sum_done", "logit_ready", "LT_done", "scan_done", "FT_done", "last_ready", "last_lo_ready",
             "ext_done", "step_done", "max_ready", "fall_ready", "max_kept", "max_lo_ready", "M_done", "above_ready",
             "weight_ready", "shrink_ready", "attr_ready", "msg_ready", "agg_done", "scaled", "added"))
        block = ctx.enter_context(nc.Block())
        first, last_turn = -3, STEPS + 3
        looped = (RING - 3, STEPS - 3)

        @block.sync
        def _(sp):
            for k, s, _ in sweep(sp, 0, RING, STEPS, STEPS, RING, UNROLL):
                if inside(k - RING, STEPS):
                    sp.wait_ge(agg_done, k - RING + 1)
                g = sp.value_load(grp_tab[0:1, one(k)], min_val=0, max_val=GROUPS - 1)
                e = sp.value_load(edge_tab[0:1, one(k)], min_val=0, max_val=E - GROUP)
                sp.dma_start(meta[:, s], meta_dram[bass.DynSlice(g, 1)].rearrange("g p m -> p (g m)")
                             ).then_inc(loads[s], 16)
                sp.dma_start(rbf[:, s], edge_attr[bass.DynSlice(e, GROUP), :].rearrange("(p t) k -> p (t k)", t=TILES)
                             ).then_inc(loads[s], 16)
                row = starts_dram[bass.DynSlice(g, 1)].rearrange("g t p -> t g p")
                sp.dma_start(starts[:, s], row.broadcast_to([TILES, HEADS, P])).then_inc(loads[s], 16)

        @block.gpsimd
        def _(pool):
            nc.gpsimd.memset(logit_all[:], 1.0).then_inc(state_ready, 1)
            nc.gpsimd.memset(run_all[:], 0.0).then_inc(state_ready, 1)
            nc.gpsimd.memset(minus_big[:], -BIG).then_inc(state_ready, 1)
            nc.gpsimd.memset(plus_big[:], BIG).then_inc(state_ready, 1)
            for k, s, r in sweep(pool, 0, RING, STEPS, STEPS, RING, UNROLL):
                full = settled(pool, (r + 1) * FULL)
                pool.wait_ge(state_ready, 4)
                pool.wait_ge(loads[s], full)
                for t in range(TILES):
                    pool.indirect_dma_start(out=xl_g[:, s, t], out_offset=None, in_=xl_table,
                                            in_offset=bass.IndirectOffsetOnAxis(ap=meta[:, s, t:t + 1], axis=0)
                                            ).then_inc(gathers[s], 16)

        @block.tensor
        def _(pe):
            for k, s, r in sweep(pe, first, *looped, last_turn, RING, UNROLL):
                if inside(k + 2, STEPS):
                    pe.wait_ge(oh_ready, k + 3)
                    if inside(k + 1, STEPS):
                        pe.wait_ge(rbfT_ready, k + 2)
                    for t in range(TILES):
                        nc.tensor.transpose(ohT_ps[:, t * P:(t + 1) * P], high(onehot[:, (s + 2) % RING, t]), ident16[:])
                    nc.tensor.transpose(rbfT_ps, rbf[:, (s + 2) % RING], ident[:]).then_inc(ohT_done, 1)
                if inside(k - 3, STEPS):
                    pe.wait_ge(msg_ready, k - 2)
                    pe.wait_ge(attr_ready, k - 2)
                    if inside(k - 4, STEPS):
                        pe.wait_ge(added, k - 3)
                    for t in range(TILES):
                        mm = nc.tensor.matmul(U_ps, onehot[:, (s - 3) % RING, t], msg[:, (s - 3) % 2, t],
                                              start=t == 0, stop=t == TILES - 1)
                    mm.then_inc(agg_done, 1)
                if inside(k - 1, STEPS):
                    pe.wait_ge(scan_done, k)
                    nc.tensor.transpose(FT_all, run_all[:], ident[0:FILLED, 0:FILLED]).then_inc(FT_done, 1)
                if inside(k - 2, STEPS):
                    pe.wait_ge(max_lo_ready, k - 1)
                    nc.tensor.matmul(M_all, ident16[:], plus_big[:], start=True, stop=False)
                    for t in range(TILES):
                        to_edges = onehotT[:, (s - 2) % 4, t * P:(t + 1) * P]
                        nc.tensor.matmul(M_ps[:, t], to_edges, minus_big[:, 0:HEADS], start=False, stop=False)
                        nc.tensor.matmul(M_ps[:, t], to_edges, high(new_max[:]), start=False, stop=False)
                        mm = nc.tensor.matmul(M_ps[:, t], to_edges, max_lo[:], start=False, stop=t == TILES - 1)
                    mm.then_inc(M_done, 1)
                if inside(k + 1, STEPS):
                    pe.wait_ge(rbfT_ready, k + 2)
                    if inside(k, STEPS):
                        pe.wait_ge(z_ready, k + 1)
                    for t in range(0, TILES, 2):
                        nc.tensor.matmul(z_ps[:, t:t + 2, 0:ROW], rbfT[:, (s + 1) % 2],
                                         Wc_diag[:, t * ROW:(t + 2) * ROW], start=True, stop=False)
                if inside(k + 1, STEPS):
                    w = pe.value_load(win_tab[0:1, one(k + 1)], min_val=0, max_val=WINDOWS - 1)
                if inside(k - 1, STEPS):
                    pe.wait_ge(last_lo_ready, k)
                    nc.tensor.matmul(ext_all, ident16[:], minus_big[:], start=True, stop=False)
                    for t in range(TILES):
                        to_nodes = high(onehot[:, (s - 1) % RING, t])
                        flag = high(meta[:, (s - 1) % RING, 2 * TILES + t:2 * TILES + t + 1])
                        nc.tensor.matmul(ext_ps[:, t], to_nodes, flag.broadcast_to([P, HEADS]), start=False, stop=False)
                        nc.tensor.matmul(ext_ps[:, t], to_nodes, high(last_max[:, t]), start=False, stop=False)
                        mm = nc.tensor.matmul(ext_ps[:, t], to_nodes, last_lo[:, t], start=False, stop=t == TILES - 1)
                    mm.then_inc(ext_done, 1)
                if inside(k + 1, STEPS):
                    pe.wait_ge(ohT_ready, k + 2)
                for half in (0, 1):
                    if inside(k + 1, STEPS):
                        for t in (2 * half, 2 * half + 1):
                            for part in range(PARTS):
                                mm = nc.tensor.matmul(z_ps[:, t, 0:ROW], onehotT[:, (s + 1) % 4, t * P:(t + 1) * P],
                                                      parts_of(xr_parts, w, part),
                                                      start=False, stop=t % 2 == 1 and part == PARTS - 1)
                    if half == 0 and inside(k, STEPS):
                        full = settled(pe, k + 1)
                        pe.wait_ge(state_ready, 4)
                        pe.wait_ge(logit_ready, full)
                        nc.tensor.transpose(LT_all, logit_all[:, s % 2], ident[:]).then_inc(LT_done, 1)
                if inside(k + 1, STEPS):
                    mm.then_inc(z_done, 1)

        @block.scalar
        def _(act):
            for k, s, r in sweep(act, first, *looped, last_turn, RING, UNROLL):
                if inside(k + 3, STEPS):
                    s3, r3 = (s + 3) % RING, r + (s + 3) // RING
                    act.wait_ge(loads[s3], (r3 + 1) * FULL)
                    nc.scalar.activation(minus_slot[:], meta[:, s3, TILES:2 * TILES].bitcast(FP32), ACT.Identity,
                                         scale=-1.0, bias=base_tab[:, one(k + 3)]).then_inc(slot_ready, 1)
                if inside(k - 2, STEPS):
                    if inside(k - 4, STEPS):
                        act.wait_ge(agg_done, k - 3)
                    nc.scalar.activation(msg[:, s % 2, :, CNT:AGG],
                                         rbf[:, (s - 2) % RING].rearrange("p (t k) -> p t k", t=TILES), ACT.Copy
                                         ).then_inc(attr_ready, 1)
                if inside(k + 3, STEPS):
                    act.wait_ge(slot_ready, k + 4)
                    for t in range(TILES):
                        nc.scalar.activation(distance[:, t], iota_n[:], ACT.Abs, bias=minus_slot[:, t:t + 1]
                                             ).then_inc(dist_ready, 1)
                if inside(k - 2, STEPS):
                    act.wait_ge(fall_ready, k - 1)
                    nc.scalar.activation(shrink[:, s % 2], fall[:, s % 2], ACT.Exp).then_inc(shrink_ready, 1)
                if inside(k + 3, STEPS):
                    act.wait_ge(dist_ready, (k + 4) * TILES)
                    nc.scalar.activation(onehot[:, (s + 3) % RING], distance[:], ACT.Relu, scale=-1.0, bias=1.0
                                         ).then_inc(oh_ready, 1)
                if inside(k - 2, STEPS):
                    act.wait_ge(above_ready, k - 1)
                    nc.scalar.activation(msg[:, s % 2, :, 0:MSG].rearrange("p t (h c) -> p t h c", c=HC)[:, :, :, D_HEAD],
                                         above[:], ACT.Exp).then_inc(weight_ready, 1)
                if inside(k + 2, STEPS):
                    act.wait_ge(ohT_done, k + 3)
                    nc.scalar.activation(onehotT[:, (s + 2) % 4], ohT_ps, ACT.Copy).then_inc(ohT_ready, 1)
                    nc.scalar.activation(rbfT[:, s % 2], rbfT_ps, ACT.Copy).then_inc(rbfT_ready, 1)

        @block.vector
        def _(dve):
            nc.vector.memset(acc[:], 0.0).then_inc(scaled, 1)
            nc.vector.memset(node_max[:], -BIG).then_inc(max_kept, 1)
            nc.vector.memset(msg[:, :, :, MSG:CNT], 1.0).then_inc(ones_set, 1)
            dve.wait_ge(state_ready, 4)
            dve.wait_ge(ones_set, 1)
            window, written_out = {}, True
            for k, s, r in sweep(dve, first, *looped, last_turn, RING, UNROLL):
                for back in (3, 2) if isinstance(k, int) != written_out else ():
                    if inside(k - back, STEPS):
                        window[(s - back) % RING] = dve.value_load(win_tab[0:1, one(k - back)], min_val=0, max_val=WINDOWS - 1)
                written_out = isinstance(k, int)
                if inside(k, STEPS):
                    dve.wait_ge(z_done, k + 1)
                    dve.wait_ge(gathers[s], (r + 1) * GATHERED)
                    nc.vector.tensor_tensor(z[:, s % 2], z_ps[:, :, 0:ROW], xl_g[:, s], ALU.add).then_inc(z_ready, 1)
                if inside(k - 2, STEPS):
                    dve.wait_ge(max_ready, k - 1)
                    nc.vector.tensor_tensor(max_lo[:], new_max[:], high(new_max[:]), ALU.subtract
                                            ).then_inc(max_lo_ready, 1)
                    w_max = window[(s - 2) % RING]
                    nc.vector.tensor_tensor(fall[:, s % 2], at(node_max, w_max), new_max[:], ALU.subtract
                                            ).then_inc(fall_ready, 1)
                if inside(k - 1, STEPS):
                    dve.wait_ge(LT_done, k)
                    nc.vector.tensor_tensor_scan(run_max, starts[:, (s - 1) % RING], LT_ps, -BIG, ALU.add, ALU.max
                                                 ).then_inc(scan_done, 1)
                if inside(k - 2, STEPS):
                    dve.wait_ge(fall_ready, k - 1)
                    nc.vector.tensor_scalar(at(node_max, w_max), new_max[:], 1.0, None, ALU.mult).then_inc(max_kept, 1)
                if inside(k, STEPS):
                    dve.wait_ge(z_ready, k + 1)
                    nc.vector.scalar_tensor_tensor(out=u_att[:], in0=z[:, s % 2, :, 0:D_MSG], scalar=0.0,
                                                   in1=att_relu[:].unsqueeze(1).broadcast_to([P, TILES, D_MSG]),
                                                   op0=ALU.max, op1=ALU.mult).then_inc(att_done, 1)
                if inside(k - 1, STEPS):
                    dve.wait_ge(FT_done, k)
                    flags = meta[:, (s - 1) % RING, 2 * TILES:META].bitcast(FP32)
                    nc.vector.scalar_tensor_tensor(out=last_max[:], in0=flags.unsqueeze(2).broadcast_to([P, TILES, HEADS]),
                                                   scalar=1.0 / BIG, in1=FT_ps, op0=ALU.mult, op1=ALU.mult
                                                   ).then_inc(last_ready, 1)
                if inside(k - 2, STEPS):
                    dve.wait_ge(M_done, k - 1)
                    nc.vector.tensor_tensor(above[:], logit[s % 2], M_ps, ALU.subtract).then_inc(above_ready, 1)
                if inside(k - 1, STEPS):
                    dve.wait_ge(last_ready, k)
                    nc.vector.tensor_tensor(last_lo[:], last_max[:], high(last_max[:].rearrange("p t h -> p (t h)")
                                            ).rearrange("p (t h) -> p t h", h=HEADS), ALU.subtract
                                            ).then_inc(last_lo_ready, 1)
                if inside(k, STEPS):
                    dve.wait_ge(att_done, k + 1)
                    nc.vector.tensor_reduce(u_sum[:], u_att[:].rearrange("p t (h d) -> p t h d", d=D_HEAD),
                                            AX.X, ALU.add).then_inc(sum_done, 1)
                if inside(k - 1, STEPS):
                    window[(s - 1) % RING] = dve.value_load(win_tab[0:1, one(k - 1)], min_val=0, max_val=WINDOWS - 1)
                if inside(k - 3, STEPS):
                    w_sum = window[(s - 3) % RING]
                    dve.wait_ge(shrink_ready, k - 2)
                    if not inside(k - 1, STEPS):
                        dve.wait_ge(added, k - 3)
                    a = acc[:, one(w_sum), 0:MSG].rearrange("p a (h c) -> p (a h) c", c=HC)
                    nc.vector.tensor_tensor(a, a, shrink[:, (s - 3) % 2].unsqueeze(2).broadcast_to([P, HEADS, HC]),
                                            ALU.mult).then_inc(scaled, 1)
                if inside(k, STEPS):
                    dve.wait_ge(sum_done, k + 1)
                    nc.vector.tensor_tensor(logit[s % 2], u_sum[:], z[:, s % 2, :, D_MSG:ROW], ALU.add
                                            ).then_inc(logit_ready, 1)
                if inside(k - 3, STEPS):
                    dve.wait_ge(scaled, k - 1)
                    dve.wait_ge(agg_done, k - 2)
                    nc.vector.tensor_tensor(at(acc, w_sum), at(acc, w_sum), U_ps, ALU.add).then_inc(added, 1)
                if inside(k - 1, STEPS):
                    dve.wait_ge(ext_done, k)
                    nc.vector.tensor_reduce(step_max[:], ext_ps.rearrange("p t h -> p h t"), AX.X, ALU.max
                                            ).then_inc(step_done, 1)
                if inside(k - 2, STEPS):
                    dve.wait_ge(weight_ready, k - 1)
                    m = msg[:, s % 2, :, 0:MSG].rearrange("p t (h c) -> p t h c", c=HC)
                    nc.vector.tensor_tensor(m[:, :, :, 0:D_HEAD],
                                            xl_g[:, (s - 2) % RING, :, 0:D_MSG].rearrange("p t (h d) -> p t h d", d=D_HEAD),
                                            m[:, :, :, D_HEAD:HC].broadcast_to([P, TILES, HEADS, D_HEAD]), ALU.mult
                                            ).then_inc(msg_ready, 1)
                if inside(k - 1, STEPS):
                    dve.wait_ge(step_done, k)
                    nc.vector.tensor_tensor(new_max[:], step_max[:], at(node_max, window[(s - 1) % RING]), ALU.max).then_inc(max_ready, 1)


def finale(nc, banks, x, xl_table, both_table, ident, att_relu, Wc_diag, W_outT, bias_col, acc, node_max, out):
    with ExitStack() as ctx:
        def sb(name, shape, dt=FP32):
            return ctx.enter_context(nc.sbuf_tensor(name, shape, dt))

        def sem(name):
            return ctx.enter_context(nc.semaphore(name))

        x_in = sb("x_in", [P, 2, FB, D_NODE])
        xl_in = sb("xl_in", [P, 2, FB, ROW])
        both_in = sb("both_in", [P, 2, FB, ROW])
        deg = sb("deg", [P, FB])
        inv_deg = sb("inv_deg", [P, FB])
        mean = sb("mean", [P, FB, D_RBF])
        meanT = sb("meanT", [D_RBF, FB, P])
        u_att = sb("u_att_loop", [P, FB, D_MSG])
        u_sum = sb("u_sum_loop", [P, FB, HEADS])
        loop_logit = sb("loop_logit", [P, FB, HEADS])
        top = sb("top", [P, FB, HEADS])
        falls = sb("falls", [P, 2, FB, HEADS])
        weights = sb("weights", [P, 2, FB, HEADS])
        old = sb("old", [P, FB, D_MSG])
        own = sb("own", [P, FB, D_MSG])
        z = sb("z_loop", [P, FB, ROW])
        two = sb("two", [P, FB, D_MSG])
        gat = sb("gat", [P, FB, D_MSG])
        total_old = sb("total_old", [P, FB, HEADS])
        total = sb("total", [P, FB, HEADS])
        inv_total = sb("inv_total", [P, FB, HEADS])
        gatT = sb("gatT", [P, FB, P])
        result = sb("result", [P, 2, FB, D_NODE])

        (tail_zero, tail_loaded, z_added, y_copied, deg_done, inv_done, mean_done, meanT_done, meanT_ready, z_done, att_done, sum_done, logit_done,
         top_done, falls_done, weights_done, old_done, own_done, two_done, told_done, total_done, itotal_done,
         gat_done, gatT_done, gatT_ready, y_done, result_ready) = map(sem, (
             "tail_zero", "tail_loaded", "z_added", "y_copied", "deg_done", "inv_done", "mean_done", "meanT_done", "meanT_ready", "zl_done", "attl_done",
             "suml_done", "logitl_done", "top_done", "falls_done", "weights_done", "old_done", "own_done",
             "two_done", "told_done", "total_done", "itotal_done", "gat_done", "gatT_done", "gatT_ready",
             "y_done", "result_ready"))
        both_loaded, xl_loaded, x_loaded = ([sem(f"{name}_loaded{i}") for i in (0, 1)] for name in ("both", "xl", "x"))
        written = [sem(f"written{i}") for i in (0, 1)]
        block = ctx.enter_context(nc.Block())

        T_ps = banks[:, 0:2].rearrange("p b (w d) -> p (b w) d", d=P)
        z_ps = banks[:, 2:6].rearrange("p b (w d) -> p (b w) d", d=256)
        y_ps = banks[:, 6:8].rearrange("p b (w d) -> p (b w) d", d=D_NODE)
        halves = ((0, 4), (4, FB))
        turns = (-1, 1, FBATCH - 1, FBATCH, 2, 2)

        def span(tile, b):
            return tile[:, bass.DynSlice(b * FB, FB)]

        @block.sync
        def _(sp):
            def rows(table, b, n=FB):
                return table[bass.DynSlice(b * (FB * P), n * P), :].rearrange("(w p) d -> p w d", p=P)

            def load_both(b):
                sp.dma_start(both_in[:, b % 2], rows(both_table, b)).then_inc(both_loaded[b % 2], 16)

            def load_xl(b):
                sp.dma_start(xl_in[:, b % 2], rows(xl_table, b)).then_inc(xl_loaded[b % 2], 16)

            def load_x(b, n=FB):
                sp.dma_start(x_in[:, b % 2, 0:n], rows(x, b, n)).then_inc(x_loaded[b % 2], 16)

            for b in (0, 1):
                load_both(b)
                load_xl(b)
                load_x(b)
            for b in range(FBATCH):
                if b + 2 < FBATCH:
                    sp.wait_ge(z_added, b + 1)
                    load_both(b + 2)
                    sp.wait_ge(own_done, b + 1)
                    load_xl(b + 2)
                sp.wait_ge(result_ready, 2 * (b + 1))
                whole = FB if b < FBATCH - 1 else FB - 1
                sp.dma_start(rows(out, b, whole), result[:, b % 2, 0:whole]).then_inc(written[b % 2], 16)
                if b + 2 < FBATCH - 1:
                    load_x(b + 2)
                elif b + 2 == FBATCH - 1:
                    sp.wait_ge(tail_zero, 1)
                    load_x(b + 2, FB - 1)
                    sp.dma_start(x_in[0:LAST_ROWS, b % 2, FB - 1], x[N - LAST_ROWS:N, :]).then_inc(tail_loaded, 16)
            sp.dma_start(out[N - LAST_ROWS:N, :], result[0:LAST_ROWS, (FBATCH - 1) % 2, FB - 1]
                         ).then_inc(written[(FBATCH - 1) % 2], 16)
            for i in (0, 1):
                sp.wait_ge(written[i], 16 * (len(range(i, FBATCH, 2)) + (i == (FBATCH - 1) % 2)))

        @block.gpsimd
        def _(pool):
            for b, s, r in sweep(pool, 0, *turns[1:]):
                if isinstance(b, int) and b == FBATCH - 2:
                    pool.wait_ge(result_ready, 2 * b)
                    nc.gpsimd.memset(x_in[:, (FBATCH - 1) % 2, FB - 1], 0.0).then_inc(tail_zero, 1)
                pool.wait_ge(x_loaded[s], (r + 1) * 16)
                if isinstance(b, int) and b == FBATCH - 1:
                    pool.wait_ge(tail_loaded, 16)
                for half, (lo, hi) in enumerate(halves):
                    pool.wait_ge(y_copied, b * 2 + half + 1)
                    nc.gpsimd.tensor_tensor(result[:, s, lo:hi], result[:, s, lo:hi], x_in[:, s, lo:hi], ALU.add
                                            ).then_inc(result_ready, 1)

        @block.tensor
        def _(pe):
            for b, s, r in sweep(pe, *turns):
                n = b + 1
                if inside(n, FBATCH):
                    pe.wait_ge(mean_done, n + 1)
                    if inside(b - 1, FBATCH):
                        pe.wait_ge(gatT_ready, b)
                    for i in range(FB):
                        mm = nc.tensor.transpose(T_ps[0:D_RBF, i], mean[:, i], ident[:])
                    mm.then_inc(meanT_done, 1)
                    if inside(b, FBATCH):
                        pe.wait_ge(z_added, n)
                    pe.wait_ge(meanT_ready, n + 1)
                    for i in range(FB):
                        mm = nc.tensor.matmul(z_ps[:, i, 0:ROW], meanT[:, i], Wc_diag[0:D_RBF, 0:ROW],
                                              start=True, stop=True)
                    mm.then_inc(z_done, 1)
                if inside(b, FBATCH):
                    pe.wait_ge(gat_done, b + 1)
                    for i in range(FB):
                        mm = nc.tensor.transpose(T_ps[:, i], gat[:, i], ident[:])
                    mm.then_inc(gatT_done, 1)
                    pe.wait_ge(gatT_ready, b + 1)
                    for half, (lo, hi) in enumerate(halves):
                        if half or inside(b - 1, FBATCH):
                            pe.wait_ge(y_copied, b * 2 + half)
                        for i in range(lo, hi):
                            mm = nc.tensor.matmul(y_ps[:, i - lo], gatT[:, i], W_outT[:], start=True, stop=True)
                        mm.then_inc(y_done, 1)

        @block.scalar
        def _(act):
            for b, s, r in sweep(act, *turns):
                n = b + 1
                if inside(n, FBATCH):
                    act.wait_ge(meanT_done, n + 1)
                    nc.scalar.activation(meanT[:], T_ps[0:D_RBF, 0:FB], ACT.Copy).then_inc(meanT_ready, 1)
                if inside(b, FBATCH):
                    act.wait_ge(gatT_done, b + 1)
                    nc.scalar.activation(gatT[:], T_ps[:, 0:FB], ACT.Identity, bias=bias_col[:]).then_inc(gatT_ready, 1)
                if inside(n, FBATCH):
                    act.wait_ge(falls_done, n * 2 + 2)
                    nc.scalar.activation(weights[:], falls[:], ACT.Exp).then_inc(weights_done, 1)
                if inside(b, FBATCH):
                    if inside(b - 2, FBATCH):
                        act.wait_ge(written[s], r * 16)
                    for half, (lo, hi) in enumerate(halves):
                        act.wait_ge(y_done, b * 2 + half + 1)
                        nc.scalar.activation(result[:, s, lo:hi], y_ps[:, 0:hi - lo], ACT.Copy
                                             ).then_inc(y_copied, 1)

        @block.vector
        def _(dve):
            def heads(ap):
                return ap.rearrange("p w (h d) -> p w h d", h=HEADS)

            def spread(ap):
                return ap.unsqueeze(3).broadcast_to([P, FB, HEADS, D_HEAD])

            for b, s, r in sweep(dve, *turns):
                n, n_s = b + 1, (s + 1) % 2
                n_r = r + (s + 1) // 2
                if inside(n, FBATCH):
                    a = span(acc, n)
                    if inside(b, FBATCH):
                        dve.wait_ge(meanT_done, n)
                    nc.vector.tensor_scalar(deg[:], a[:, :, MSG], 1.0, None, ALU.max).then_inc(deg_done, 1)
                    dve.wait_ge(deg_done, n + 1)
                    nc.vector.reciprocal(inv_deg[:], deg[:]).then_inc(inv_done, 1)
                    dve.wait_ge(inv_done, n + 1)
                    nc.vector.tensor_tensor(mean[:], a[:, :, CNT:AGG],
                                            inv_deg[:].unsqueeze(2).broadcast_to([P, FB, D_RBF]), ALU.mult
                                            ).then_inc(mean_done, 1)
                if inside(b, FBATCH):
                    sums = span(acc, b)[:, :, 0:MSG].rearrange("p w (h c) -> p w h c", c=HC)
                    dve.wait_ge(weights_done, b + 1)
                    nc.vector.tensor_tensor(total_old[:], sums[:, :, :, D_HEAD], weights[:, 0], ALU.mult
                                            ).then_inc(told_done, 1)
                    nc.vector.tensor_tensor(heads(old[:]), sums[:, :, :, 0:D_HEAD], spread(weights[:, 0]), ALU.mult
                                            ).then_inc(old_done, 1)
                    dve.wait_ge(told_done, b + 1)
                    nc.vector.tensor_tensor(total[:], total_old[:], weights[:, 1], ALU.add).then_inc(total_done, 1)
                    dve.wait_ge(xl_loaded[s], (r + 1) * 16)
                    nc.vector.tensor_tensor(heads(own[:]), heads(xl_in[:, s, :, 0:D_MSG]), spread(weights[:, 1]),
                                            ALU.mult).then_inc(own_done, 1)
                    dve.wait_ge(total_done, b + 1)
                    nc.vector.reciprocal(inv_total[:], total[:]).then_inc(itotal_done, 1)
                    dve.wait_ge(old_done, b + 1)
                    dve.wait_ge(own_done, b + 1)
                    nc.vector.tensor_tensor(two[:], old[:], own[:], ALU.add).then_inc(two_done, 1)
                    dve.wait_ge(two_done, b + 1)
                    dve.wait_ge(itotal_done, b + 1)
                    if inside(b - 1, FBATCH):
                        dve.wait_ge(gatT_done, b)
                    nc.vector.tensor_tensor(heads(gat[:]), heads(two[:]), spread(inv_total[:]), ALU.mult
                                            ).then_inc(gat_done, 1)
                if inside(n, FBATCH):
                    dve.wait_ge(z_done, n + 1)
                    dve.wait_ge(both_loaded[n_s], (n_r + 1) * 16)
                    nc.vector.tensor_tensor(z[:], z_ps[:, 0:FB, 0:ROW], both_in[:, n_s], ALU.add).then_inc(z_added, 1)
                    dve.wait_ge(z_added, n + 1)
                    nc.vector.scalar_tensor_tensor(out=u_att[:], in0=z[:, :, 0:D_MSG], scalar=0.0,
                                                   in1=att_relu[:].unsqueeze(1).broadcast_to([P, FB, D_MSG]),
                                                   op0=ALU.max, op1=ALU.mult).then_inc(att_done, 1)
                    dve.wait_ge(att_done, n + 1)
                    nc.vector.tensor_reduce(u_sum[:], heads(u_att[:]), AX.X, ALU.add).then_inc(sum_done, 1)
                    dve.wait_ge(sum_done, n + 1)
                    nc.vector.tensor_tensor(loop_logit[:], u_sum[:], z[:, :, D_MSG:ROW], ALU.add
                                            ).then_inc(logit_done, 1)
                    dve.wait_ge(logit_done, n + 1)
                    nc.vector.tensor_tensor(top[:], loop_logit[:], span(node_max, n), ALU.max).then_inc(top_done, 1)
                    dve.wait_ge(top_done, n + 1)
                    nc.vector.tensor_tensor(falls[:, 0], span(node_max, n), top[:], ALU.subtract
                                            ).then_inc(falls_done, 1)
                    nc.vector.tensor_tensor(falls[:, 1], loop_logit[:], top[:], ALU.subtract).then_inc(falls_done, 1)


_INS = ["x", "src", "dst", "edge_attr_32"] + ["L0_gnn_" + n for n in (
    "W_n2m", "W_r2m", "Wl", "bl", "Wr", "br", "We", "att", "bias", "W_m2n")]


def kernel(**inputs):
    import concourse.bacc as bacc
    from concourse.bass_utils import run_bass_kernel_spmd as run

    nc = bacc.Bacc("TRN2", target_bir_lowering=False, num_devices=1)
    arrays, args = {}, []
    for name in _INS:
        a = np.ascontiguousarray(inputs[name])
        arrays[f"in_{name}"] = a
        args.append(nc.dram_tensor(f"in_{name}", a.shape, mybir.dt.from_np(a.dtype), kind="ExternalInput").ap())
    args.append(nc.dram_tensor("out_0", (N, D_NODE), FP32, kind="ExternalOutput").ap())
    gat_kernel(nc, *args)
    return run(nc, [arrays], core_ids=[0]).results[0]["out_0"]
```
